# Optimizing a Trainium2 kernel written in Bass

```python
import numpy as np
import jax
import jax.numpy as jnp

def _softmax(x, axis=-1):
    return jax.nn.softmax(x, axis=axis)

def _gelu(x):
    return jax.nn.gelu(x, approximate=True)

def _silu(x):
    return jax.nn.silu(x)

def _sigmoid(x):
    return jax.nn.sigmoid(x)

def _layernorm(x, axis=-1, eps=1e-05):
    m = jnp.mean(x, axis=axis, keepdims=True)
    v = jnp.var(x, axis=axis, keepdims=True)
    return (x - m) / jnp.sqrt(v + eps)

def _scatter_add(tgt, idx, src, axis=0):
    return tgt.at[idx].add(src)

def _segment_sum(src, seg, n):
    return jax.ops.segment_sum(src, seg, n)
kernel_name = 'mk_dlrm_tower_d1_rec_r8_d074cc'

def setup_inputs(seed: int=0):
    np.random.seed(seed)
    _w = jnp.asarray

    def _rec_inputs():
        import jax
        import jax.numpy as jnp
        _tk = jax.random.key(seed)
        ids = jnp.stack([jax.random.randint(jax.random.fold_in(_tk, 200 + f), (512,), 0, v, jnp.int32) for f, v in enumerate([125000, 12500, 1250, 1000, 1000, 1000, 12500, 1000, 1000, 1250, 1000, 12500, 1250, 1250, 12500, 12500, 1250, 1250, 12500, 12500, 1000, 1250, 12500, 1250, 1000, 1000])], axis=1)
        tbl_0 = 0.05 * jax.random.normal(jax.random.fold_in(_tk, 500 + 0), (125000, 128), jnp.float32)
        tbl_1 = 0.05 * jax.random.normal(jax.random.fold_in(_tk, 500 + 1), (12500, 128), jnp.float32)
        tbl_2 = 0.05 * jax.random.normal(jax.random.fold_in(_tk, 500 + 2), (1250, 128), jnp.float32)
        tbl_3 = 0.05 * jax.random.normal(jax.random.fold_in(_tk, 500 + 3), (1000, 128), jnp.float32)
        tbl_4 = 0.05 * jax.random.normal(jax.random.fold_in(_tk, 500 + 4), (1000, 128), jnp.float32)
        tbl_5 = 0.05 * jax.random.normal(jax.random.fold_in(_tk, 500 + 5), (1000, 128), jnp.float32)
        tbl_6 = 0.05 * jax.random.normal(jax.random.fold_in(_tk, 500 + 6), (12500, 128), jnp.float32)
        tbl_7 = 0.05 * jax.random.normal(jax.random.fold_in(_tk, 500 + 7), (1000, 128), jnp.float32)
        tbl_8 = 0.05 * jax.random.normal(jax.random.fold_in(_tk, 500 + 8), (1000, 128), jnp.float32)
        tbl_9 = 0.05 * jax.random.normal(jax.random.fold_in(_tk, 500 + 9), (1250, 128), jnp.float32)
        tbl_10 = 0.05 * jax.random.normal(jax.random.fold_in(_tk, 500 + 10), (1000, 128), jnp.float32)
        tbl_11 = 0.05 * jax.random.normal(jax.random.fold_in(_tk, 500 + 11), (12500, 128), jnp.float32)
        tbl_12 = 0.05 * jax.random.normal(jax.random.fold_in(_tk, 500 + 12), (1250, 128), jnp.float32)
        tbl_13 = 0.05 * jax.random.normal(jax.random.fold_in(_tk, 500 + 13), (1250, 128), jnp.float32)
        tbl_14 = 0.05 * jax.random.normal(jax.random.fold_in(_tk, 500 + 14), (12500, 128), jnp.float32)
        tbl_15 = 0.05 * jax.random.normal(jax.random.fold_in(_tk, 500 + 15), (12500, 128), jnp.float32)
        tbl_16 = 0.05 * jax.random.normal(jax.random.fold_in(_tk, 500 + 16), (1250, 128), jnp.float32)
        tbl_17 = 0.05 * jax.random.normal(jax.random.fold_in(_tk, 500 + 17), (1250, 128), jnp.float32)
        tbl_18 = 0.05 * jax.random.normal(jax.random.fold_in(_tk, 500 + 18), (12500, 128), jnp.float32)
        tbl_19 = 0.05 * jax.random.normal(jax.random.fold_in(_tk, 500 + 19), (12500, 128), jnp.float32)
        tbl_20 = 0.05 * jax.random.normal(jax.random.fold_in(_tk, 500 + 20), (1000, 128), jnp.float32)
        tbl_21 = 0.05 * jax.random.normal(jax.random.fold_in(_tk, 500 + 21), (1250, 128), jnp.float32)
        tbl_22 = 0.05 * jax.random.normal(jax.random.fold_in(_tk, 500 + 22), (12500, 128), jnp.float32)
        tbl_23 = 0.05 * jax.random.normal(jax.random.fold_in(_tk, 500 + 23), (1250, 128), jnp.float32)
        tbl_24 = 0.05 * jax.random.normal(jax.random.fold_in(_tk, 500 + 24), (1000, 128), jnp.float32)
        tbl_25 = 0.05 * jax.random.normal(jax.random.fold_in(_tk, 500 + 25), (1000, 128), jnp.float32)
        _rk = jax.random.fold_in(_tk, 7)
        r_bottom_output = -0.000520686 + 1.00062 * jax.random.normal(jax.random.fold_in(_rk, 101), (512, 128), jnp.float32)
        W_top1 = 0.0456912 * jax.random.normal(jax.random.fold_in(_tk, 801), (479, 512), jnp.float32)
        W_top2 = 0.0441942 * jax.random.normal(jax.random.fold_in(_tk, 802), (512, 256), jnp.float32)
        W_top3 = 0.0625 * jax.random.normal(jax.random.fold_in(_tk, 803), (256, 1), jnp.float32)
        b_top1 = jnp.zeros((512,), jnp.float32)
        b_top2 = jnp.zeros((256,), jnp.float32)
        return (r_bottom_output, ids, tbl_0, tbl_1, tbl_2, tbl_3, tbl_4, tbl_5, tbl_6, tbl_7, tbl_8, tbl_9, tbl_10, tbl_11, tbl_12, tbl_13, tbl_14, tbl_15, tbl_16, tbl_17, tbl_18, tbl_19, tbl_20, tbl_21, tbl_22, tbl_23, tbl_24, tbl_25, W_top1, b_top1, W_top2, b_top2, W_top3)
    r_bottom_output, ids, tbl_0, tbl_1, tbl_2, tbl_3, tbl_4, tbl_5, tbl_6, tbl_7, tbl_8, tbl_9, tbl_10, tbl_11, tbl_12, tbl_13, tbl_14, tbl_15, tbl_16, tbl_17, tbl_18, tbl_19, tbl_20, tbl_21, tbl_22, tbl_23, tbl_24, tbl_25, W_top1, b_top1, W_top2, b_top2, W_top3 = _rec_inputs()

    def _L0_rec_setup():
        import jax, jax.numpy as jnp
        import numpy as np
        NUM_FEATURES = 27
        _TRIU_I, _TRIU_J = np.triu_indices(NUM_FEATURES, k=1)
        key = jax.random.key(seed)
        k1, k2 = jax.random.split(key)
        bottom_output = jax.random.normal(k1, (2048, 128), dtype=jnp.float32)
        embeddings = jax.random.normal(k2, (2048, 26, 128), dtype=jnp.float32)
        return {'bottom_output': bottom_output, 'embeddings': embeddings}
    _L0_rec_all = _L0_rec_setup()
    _L0_rec_in = {k: v for k, v in _L0_rec_all.items() if k in ()}
    del _L0_rec_all
    return {'r_bottom_output': r_bottom_output, 'ids': ids, 'tbl_0': tbl_0, 'tbl_1': tbl_1, 'tbl_2': tbl_2, 'tbl_3': tbl_3, 'tbl_4': tbl_4, 'tbl_5': tbl_5, 'tbl_6': tbl_6, 'tbl_7': tbl_7, 'tbl_8': tbl_8, 'tbl_9': tbl_9, 'tbl_10': tbl_10, 'tbl_11': tbl_11, 'tbl_12': tbl_12, 'tbl_13': tbl_13, 'tbl_14': tbl_14, 'tbl_15': tbl_15, 'tbl_16': tbl_16, 'tbl_17': tbl_17, 'tbl_18': tbl_18, 'tbl_19': tbl_19, 'tbl_20': tbl_20, 'tbl_21': tbl_21, 'tbl_22': tbl_22, 'tbl_23': tbl_23, 'tbl_24': tbl_24, 'tbl_25': tbl_25, 'W_top1': W_top1, 'b_top1': b_top1, 'W_top2': W_top2, 'b_top2': b_top2, 'W_top3': W_top3}

def reference(r_bottom_output, ids, tbl_0, tbl_1, tbl_2, tbl_3, tbl_4, tbl_5, tbl_6, tbl_7, tbl_8, tbl_9, tbl_10, tbl_11, tbl_12, tbl_13, tbl_14, tbl_15, tbl_16, tbl_17, tbl_18, tbl_19, tbl_20, tbl_21, tbl_22, tbl_23, tbl_24, tbl_25, W_top1, b_top1, W_top2, b_top2, W_top3):
    import jax
    import jax.numpy as jnp

    def _L0_rec_ref(bottom_output, embeddings):
        import jax, jax.numpy as jnp
        import numpy as np
        NUM_FEATURES = 27
        _TRIU_I, _TRIU_J = np.triu_indices(NUM_FEATURES, k=1)
        all_emb = jnp.concatenate([bottom_output[:, None, :], embeddings], axis=1)
        gram = jnp.einsum('bfd,bgd->bfg', all_emb, all_emb)
        return gram[:, _TRIU_I, _TRIU_J]
    e = jnp.stack([tbl_0[ids[:, 0]], tbl_1[ids[:, 1]], tbl_2[ids[:, 2]], tbl_3[ids[:, 3]], tbl_4[ids[:, 4]], tbl_5[ids[:, 5]], tbl_6[ids[:, 6]], tbl_7[ids[:, 7]], tbl_8[ids[:, 8]], tbl_9[ids[:, 9]], tbl_10[ids[:, 10]], tbl_11[ids[:, 11]], tbl_12[ids[:, 12]], tbl_13[ids[:, 13]], tbl_14[ids[:, 14]], tbl_15[ids[:, 15]], tbl_16[ids[:, 16]], tbl_17[ids[:, 17]], tbl_18[ids[:, 18]], tbl_19[ids[:, 19]], tbl_20[ids[:, 20]], tbl_21[ids[:, 21]], tbl_22[ids[:, 22]], tbl_23[ids[:, 23]], tbl_24[ids[:, 24]], tbl_25[ids[:, 25]]], axis=1)
    z = _L0_rec_ref(r_bottom_output, e)
    z = z.reshape(z.shape[0], -1)
    h = jnp.concatenate([z, r_bottom_output], axis=1)
    h = jnp.maximum(h @ W_top1 + b_top1, 0.0)
    h = jnp.maximum(h @ W_top2 + b_top2, 0.0)
    y = h @ W_top3
    return y

_drawn_inputs = setup_inputs


def setup_inputs(seed=0):
    import zlib

    import numpy as np

    out = dict(_drawn_inputs(seed))
    spreads = {'b_top1': (0.0, 0.1), 'b_top2': (0.0, 0.1)}
    factors = {}
    for name, (base, spread) in spreads.items():
        noise = np.random.default_rng([zlib.crc32(name.encode()), seed]).standard_normal(out[name].shape)
        drawn = base * np.exp(spread * noise) if base else spread * noise
        out[name] = jnp.asarray(drawn.astype(out[name].dtype))
    for name, factor in factors.items():
        out[name] = (out[name] * factor).astype(out[name].dtype)
    return out
```

```python
import concourse.bass as bass
from concourse import mybir
from contextlib import ExitStack

B = 512
D = 128
TABLES = 26
FEATURES = TABLES + 1
TILES = B // 128
LAST = TILES - 1
GROUPS = 32
BANK_GROUPS = GROUPS // 2
ROWS = COLS = FEATURES - 1
KTILES = -(-COLS // 4)
LATE = 5
LATE_COLS = COLS - 4 * LATE
BIAS_ROW = ROWS
N1, N2 = 512, 256
K2 = N1 // 128

LOOKED_UP = [3, 4, 5, 7, 8, 10, 20]
LOOKED = len(LOOKED_UP)
VOCAB = 1000
VP = 125
VK = VOCAB // VP
FIRST_CHUNKS = 4
RING = 3
HOT_RING = 14
CHUNKS = KTILES + 1 + 2
CHUNK_RING = 2 * RING
SLOT_TABLE = [None] + LOOKED_UP + [f for f in range(TABLES) if f not in LOOKED_UP]


def dve_tiles(i):
    return VK - 1 - i % 2


def act_tiles_before(i):
    return i * VK - sum(dve_tiles(j) for j in range(i))


def gathered_slots(k):
    return [g for g in range(1 + 4 * k, min(5 + 4 * k, FEATURES)) if g > LOOKED]


BANKS = [k for k in range(KTILES) if gathered_slots(k)]
EARLY = sum(k < LATE for k in BANKS)


def tower(nc, bottom, ids, hot_ids, tables, w1, w2, b2, w3, out):
    fp32, fp32r, i32 = mybir.dt.float32, mybir.dt.float32r, mybir.dt.int32
    ALU, ACT = mybir.AluOpType, mybir.ActivationFunctionType

    ctx = ExitStack()
    with ctx:
        def sb(name, shape, dt=fp32):
            return ctx.enter_context(nc.sbuf_tensor(name, shape, dt))

        def pb(name, shape):
            return ctx.enter_context(nc.psum_tensor(name, shape, fp32))

        def sem(name):
            return ctx.enter_context(nc.semaphore(name))

        idx = sb("idx", [128, TILES * TABLES], i32)
        hot = sb("hot", [VP, RING, B], i32)
        row0 = sb("row0", [VP, 1], i32)
        row0f = sb("row0f", [VP, 1])
        minus_k = sb("minus_k", [VP, 2])
        tab = sb("tab", [128, RING, VK, D])
        tab_hi = sb("tab_hi", [VP, 2, VK, D], fp32r)
        tab_lo = sb("tab_lo", [VP, 2, VK, D], fp32r)
        square = sb("square", [VP, B])
        onehot = sb("onehot", [VP, HOT_RING, B], fp32r)
        bot = sb("bot", [128, TILES, D])
        emb = sb("emb", [128, 2, TABLES - LOOKED, D])
        embT = sb("embT", [128, TILES, 128, FEATURES])
        bot_hi = sb("bot_hi", [128, TILES, 128], fp32r)
        bot_lo = sb("bot_lo", [128, TILES, 128], fp32r)
        prod = sb("prod", [128, KTILES, 128])
        prod_hi = sb("prod_hi", [128, KTILES, 128], fp32r)
        prod_lo = sb("prod_lo", [128, KTILES, 128], fp32r)
        w_hi = sb("w_hi", [128, CHUNKS, N1], fp32r)
        w_lo = sb("w_lo", [128, CHUNKS, N1], fp32r)
        b2s = sb("b2s", [1, N2])
        w3s = sb("w3s", [128, N2])
        ones = sb("ones", [128, 128])
        ident = sb("ident", [128, 128])
        h1 = sb("h1", [128, N1])
        h1T_hi = sb("h1T_hi", [128, K2, 128], fp32r)
        h1T_lo = sb("h1T_lo", [128, K2, 128], fp32r)
        h2w = sb("h2w", [128, N2])
        y = sb("y", [128, TILES])

        pT = [pb(f"pT{i}", [128, 512]) for i in range(2)]
        pG = [pb(f"pG{i}", [128, 2, 512]) for i in range(2)]
        pH1 = pb("pH1", [128, N1])
        pH2 = pb("pH2", [128, N2])

        s_ids = sem("s_ids")
        s_hotids = [sem(f"s_hotids{i}") for i in range(LOOKED)]
        s_tab = [sem(f"s_tab{i}") for i in range(LOOKED)]
        s_bot = sem("s_bot")
        s_w = [sem(f"s_w{c}") for c in range(CHUNKS)]
        s_small = sem("s_small")
        s_ident0 = sem("s_ident0")
        s_ident = sem("s_ident")
        s_row0 = sem("s_row0")
        s_row0f = sem("s_row0f")
        s_rel = sem("s_rel")
        s_ones = sem("s_ones")
        s_prod1 = sem("s_prod1")
        s_row = [[sem(f"s_row{t}_{k}") for k in BANKS] for t in range(TILES)]
        s_tabhi = sem("s_tabhi")
        s_tablo = sem("s_tablo")
        s_hotv = sem("s_hotv")
        s_sq = sem("s_sq")
        s_hota = sem("s_hota")
        s_look = sem("s_look")
        s_lookc = sem("s_lookc")
        s_bank = sem("s_bank")
        s_bankv = sem("s_bankv")
        s_banka = sem("s_banka")
        s_bothi = sem("s_bothi")
        s_botlo = sem("s_botlo")
        s_whi = sem("s_whi")
        s_wlo = sem("s_wlo")
        s_gram = sem("s_gram")
        s_gv = sem("s_gv")
        s_ga = sem("s_ga")
        s_phi = sem("s_phi")
        s_plo = sem("s_plo")
        s_l1 = sem("s_l1")
        s_h1 = sem("s_h1")
        s_h1p = sem("s_h1p")
        s_h1hi = sem("s_h1hi")
        s_h1lo = sem("s_h1lo")
        s_l2 = sem("s_l2")
        s_y = sem("s_y")
        s_out = sem("s_out")

        block = ctx.enter_context(nc.Block())

        w1_hi, w1_lo = w_hi[:, 0:KTILES + 1, :], w_lo[:, 0:KTILES + 1, :]
        w2_hi, w2_lo = (w[:, KTILES + 1:, :].rearrange("p c (k n) -> p (c k) n", n=N2) for w in (w_hi, w_lo))

        def bank_slots(t, i):
            slots = gathered_slots(BANKS[i])
            return embT[:, t, :, slots[0]:slots[-1] + 1].rearrange("d p f -> d f p")

        def bank(t, i):
            return pT[(t * len(BANKS) + i) % 2][:, 0:128 * len(gathered_slots(BANKS[i]))].rearrange(
                "d (f p) -> d f p", p=128)

        def hot_rows(i, k):
            return onehot[:, (i * VK + k) % HOT_RING, :]

        def wait_hot_free(engine, i, k):
            if i * VK + k >= HOT_RING:
                engine.wait_ge(s_look, i * VK + k - HOT_RING + 1)

        def chunk(c):
            table = (LOOKED + (c % CHUNK_RING) // 2) % RING
            return tab[:, table, VK // 2 * (c % 2):VK // 2 * (c % 2 + 1), :].rearrange("p k d -> p (k d)")

        def even(t, i):
            return (t * len(BANKS) + i) % 2 == 0

        def gram_blocks(t):
            return pG[t % 2][:, :, 0:BANK_GROUPS * COLS].rearrange("p b (i c) -> p b i c", c=COLS)

        late_blocks = pG[(LAST + 1) % 2][:, :, 0:BANK_GROUPS * LATE_COLS].rearrange(
            "p b (i c) -> p b i c", c=LATE_COLS)

        def gram_copies(copy, blocks, rows, first, k0, k1, quadrants):
            banks, groups = blocks.shape[1], blocks.shape[2]
            cols = min(4 * k1, COLS) - 4 * k0
            for s in quadrants:
                for j in range(4):
                    nk = (cols - j + 3) // 4
                    a = blocks[32 * s:32 * s + rows, :, :, j:cols:4]
                    b = prod[32 * j:32 * j + rows, k0:k0 + nk, 4 * first + s:4 * (first + banks * groups):4]
                    last = copy(b.rearrange("p k (b i) -> p b i k", b=banks), a)
            return last

        @block.sync
        def _(sp):
            def load_lookup(i):
                if i >= RING:
                    sp.wait_ge(s_look, (i - RING + 1) * VK)
                sp.dma_start(hot[:, i % RING, :], hot_ids[i:i + 1, :].broadcast_to([VP, B])).then_inc(s_hotids[i], 16)
                sp.dma_start(tab[0:VP, i % RING, :, :], tables[LOOKED_UP[i]].rearrange(
                    "(p k) d -> p k d", k=VK)).then_inc(s_tab[i], 16)

            def load_weights(c):
                if c < CHUNK_RING:
                    sp.wait_ge(s_look, (LOOKED - RING + c // 2 + 1) * VK)
                else:
                    sp.wait_ge(s_wlo, c - CHUNK_RING + 1)
                if c <= KTILES:
                    dst, src = chunk(c), w1[:, c, :]
                else:
                    dst = chunk(c).rearrange("p (k n) -> p k n", n=N2)
                    src = w2.rearrange("(k p) n -> p k n", p=128)[:, 2 * (c - KTILES - 1):2 * (c - KTILES), :]
                sp.dma_start(dst, src).then_inc(s_w[c], 16)

            sp.dma_start(idx[:, :], ids.rearrange("(p t) f -> p (t f)", t=TILES)).then_inc(s_ids, 16)
            sp.dma_start(tab[0:VP, 0, :, :], tables[LOOKED_UP[0]].rearrange(
                "(p k) d -> p k d", k=VK)).then_inc(s_tab[0], 16)
            sp.dma_start(bot[:, :, :], bottom.rearrange("(p t) d -> p t d", t=TILES)).then_inc(s_bot, 16)
            load_lookup(1)
            load_lookup(2)
            sp.dma_start(b2s[:, :], b2.unsqueeze(0)).then_inc(s_small, 16)
            sp.dma_start(w3s[:, :], w3.rearrange("n o -> o n").broadcast_to([128, N2])).then_inc(s_small, 16)
            for i in range(RING, LOOKED):
                load_lookup(i)
            for c in range(CHUNKS):
                load_weights(c)
            sp.wait_ge(s_y, TILES)
            sp.dma_start(out.rearrange("(p t) o -> p (t o)", t=TILES), y[:, :]).then_inc(s_out, 16)
            sp.wait_ge(s_out, 16)

        @block.gpsimd
        def _(pool):
            nc.gpsimd.iota(row0[:, :], [[0, 1]], base=0, channel_multiplier=VK).then_inc(s_row0, 1)
            nc.gpsimd.memset(ident[:, :], 0.0).then_inc(s_ident0, 1)
            pool.wait_ge(s_ident0, 1)
            nc.gpsimd.affine_select(out=ident[:, :], in_=ident[:, :], compare_op=ALU.not_equal, fill=1.0,
                                    base=0, pattern=[[-1, 128]], channel_multiplier=1).then_inc(s_ident, 1)
            pool.wait_ge(s_ids, 16)
            for t in range(TILES):
                for i, k in enumerate(BANKS):
                    if t >= 2:
                        pool.wait_ge(s_bank, 1 + (t - 2) * len(BANKS) + i + 1)
                    for g in gathered_slots(k):
                        f = SLOT_TABLE[g]
                        c = t * TABLES + f
                        nc.gpsimd.indirect_dma_start(
                            out=emb[:, t % 2, g - LOOKED - 1, :], out_offset=None, in_=tables[f],
                            in_offset=bass.IndirectOffsetOnAxis(ap=idx[:, c:c + 1], axis=0),
                        ).then_inc(s_row[t][i], 16)

        @block.vector
        def _(dve):
            def copy_bank(t, i):
                if even(t, i):
                    dve.wait_ge(s_bank, 1 + t * len(BANKS) + i + 1)
                    nc.vector.tensor_copy(bank_slots(t, i), bank(t, i)).then_inc(s_bankv, 1)

            def subtract(lo, whole, hi):
                return nc.vector.tensor_tensor(lo, whole, hi, ALU.subtract)

            def low_products(n, k0, k1):
                if 0 < n < TILES:
                    dve.wait_ge(s_l1, n)
                dve.wait_ge(s_gv, n + 1 if n < TILES else TILES + 2)
                dve.wait_ge(s_ga, n + 1 if n < TILES else TILES + 2)
                dve.wait_ge(s_phi, n + 1)
                subtract(prod_lo[:, k0:k1, :], prod[:, k0:k1, :], prod_hi[:, k0:k1, :]).then_inc(s_plo, 1)

            def copy_gram(t, k1):
                dve.wait_ge(s_gram, t + 1)
                if t == 0:
                    dve.wait_ge(s_prod1, 1)
                else:
                    dve.wait_ge(s_phi, t)
                    dve.wait_ge(s_plo, t)
                rows = 1 + 4 * k1 if k1 < KTILES else ROWS
                gram_copies(nc.vector.tensor_copy, gram_blocks(t), rows, 0, 0, k1, (0, 1)).then_inc(s_gv, 1)

            def low_weights(c0, c1):
                for c in range(c0, c1):
                    dve.wait_ge(s_whi, c + 1)
                    subtract(w_lo[:, c, :], chunk(c), w_hi[:, c, :]).then_inc(s_wlo, 1)

            def split_h1(t):
                dve.wait_ge(s_h1p, t + 1)
                if t > 0:
                    dve.wait_ge(s_l2, t)
                whole = pG[t % 2][:, 0, :].rearrange("p (k b) -> p k b", b=128)
                nc.vector.tensor_copy(h1T_hi[:, :, :], whole).then_inc(s_h1hi, 1)
                dve.wait_ge(s_h1hi, t + 1)
                subtract(h1T_lo[:, :, :], whole, h1T_hi[:, :, :]).then_inc(s_h1lo, 1)

            def layer3(t):
                dve.wait_ge(s_l2, t + 1)
                if t == 0:
                    dve.wait_ge(s_small, 32)
                else:
                    dve.wait_ge(s_y, t)
                nc.vector.scalar_tensor_tensor(out=h2w[:, :], in0=pH2[:, :], scalar=0.0, in1=w3s[:, :],
                                               op0=ALU.max, op1=ALU.mult, accum_out=y[:, t:t + 1]).then_inc(s_y, 1)

            for m in range(2):
                nc.vector.memset(minus_k[:, m:m + 1], -float(VK - 2 + m))
            nc.vector.memset(ones[:, :], 1.0).then_inc(s_ones, 1)
            dve.wait_ge(s_row0, 1)
            nc.vector.tensor_copy(row0f[:, :], row0[:, :]).then_inc(s_row0f, 1)
            dve.wait_ge(s_row0f, 1)
            for i in range(LOOKED):
                dve.wait_ge(s_hotids[i], 16)
                nc.vector.tensor_scalar(hot[:, i % RING, :], hot[:, i % RING, :], row0f[:, :], None,
                                        ALU.subtract).then_inc(s_rel, 1)
                dve.wait_ge(s_rel, i + 1)
                for k in range(dve_tiles(i)):
                    wait_hot_free(dve, i, k)
                    nc.vector.tensor_scalar(hot_rows(i, k), hot[:, i % RING, :], float(k), None,
                                            ALU.is_equal).then_inc(s_hotv, 1)
                dve.wait_ge(s_tabhi, i + 1)
                if i >= 2:
                    dve.wait_ge(s_look, (i - 1) * VK)
                subtract(tab_lo[:, i % 2, :, :], tab[0:VP, i % RING, :, :], tab_hi[:, i % 2, :, :]).then_inc(s_tablo, 1)
                if i >= 2:
                    copy_bank(0, i - 2)
            low_weights(0, FIRST_CHUNKS)
            for i in range(LOOKED - 2, len(BANKS)):
                copy_bank(0, i)
            dve.wait_ge(s_bothi, 1)
            subtract(bot_lo[:, :, :], embT[:, :, :, 0], bot_hi[:, :, :]).then_inc(s_botlo, 1)

            low_weights(FIRST_CHUNKS, KTILES + 1)

            for t in range(LAST):
                if t > 0:
                    split_h1(t - 1)
                copy_gram(t, KTILES)
                copy_bank(t + 1, 0)
                low_products(t, 0, KTILES)
                copy_bank(t + 1, 1)
                if t > 0:
                    layer3(t - 1)
                else:
                    low_weights(KTILES + 1, CHUNKS)
                for i in range(2, EARLY if t + 1 == LAST else len(BANKS)):
                    copy_bank(t + 1, i)
            split_h1(LAST - 1)
            copy_gram(LAST, LATE)
            for i in range(EARLY, len(BANKS)):
                copy_bank(LAST, i)
            low_products(LAST, 0, LATE)
            layer3(LAST - 1)
            for h in range(2):
                dve.wait_ge(s_gram, TILES + h + 1)
                gram_copies(nc.vector.tensor_copy, late_blocks[:, h:h + 1, :, :], ROWS, h * BANK_GROUPS,
                            LATE, KTILES, (0, 1)).then_inc(s_gv, 1)
            low_products(TILES, LATE, KTILES)
            split_h1(LAST)
            layer3(LAST)

        @block.scalar
        def _(act):
            def copy_bank(t, i):
                if not even(t, i):
                    act.wait_ge(s_bank, 1 + t * len(BANKS) + i + 1)
                    nc.scalar.copy(bank_slots(t, i), bank(t, i)).then_inc(s_banka, 1)

            def start_lookup(i):
                act.wait_ge(s_tab[i], 16)
                if i >= 2:
                    act.wait_ge(s_look, (i - 1) * VK)
                nc.scalar.copy(tab_hi[:, i % 2, :, :], tab[0:VP, i % RING, :, :]).then_inc(s_tabhi, 1)
                act.wait_ge(s_rel, i + 1)
                for k in range(dve_tiles(i), VK):
                    n = act_tiles_before(i) + k - dve_tiles(i)
                    if n > 0:
                        act.wait_ge(s_hota, n)
                    nc.scalar.activation(square[:, :], hot[:, i % RING, :], ACT.Square,
                                         bias=minus_k[:, k - VK + 2:k - VK + 3]).then_inc(s_sq, 1)
                    act.wait_ge(s_sq, n + 1)
                    wait_hot_free(act, i, k)
                    nc.scalar.activation(hot_rows(i, k), square[:, :], ACT.Relu,
                                         bias=ones[0:VP, 0:1], scale=-1.0).then_inc(s_hota, 1)

            def high_weights(c0, c1):
                for c in range(c0, c1):
                    act.wait_ge(s_w[c], 16)
                    nc.scalar.copy(w_hi[:, c, :], chunk(c)).then_inc(s_whi, 1)

            def high_products(n, k0, k1):
                if n > 0:
                    act.wait_ge(s_l1, n)
                act.wait_ge(s_gv, n + 1)
                act.wait_ge(s_ga, n + 1)
                nc.scalar.copy(prod_hi[:, k0:k1, :], prod[:, k0:k1, :]).then_inc(s_phi, 1)

            def copy_gram(t, k1):
                act.wait_ge(s_gram, t + 1)
                if t == 0:
                    act.wait_ge(s_prod1, 1)
                else:
                    act.wait_ge(s_phi, t)
                    act.wait_ge(s_plo, t)
                rows = 1 + 4 * k1 if k1 < KTILES else ROWS
                gram_copies(nc.scalar.copy, gram_blocks(t), rows, 0, 0, k1, (2, 3)).then_inc(s_ga, 1)

            def relu(t):
                act.wait_ge(s_l1, t + 1)
                if t > 0:
                    act.wait_ge(s_h1p, t)
                nc.scalar.activation(h1[:, :], pH1[:, :], ACT.Relu).then_inc(s_h1, 1)

            act.dma_start(hot[:, 0, :], hot_ids[0:1, :].broadcast_to([VP, B])).then_inc(s_hotids[0], 16)
            act.wait_ge(s_ones, 1)
            nc.scalar.copy(prod[:, :, :], ones[:, :].unsqueeze(1).broadcast_to([128, KTILES, 128])).then_inc(s_prod1, 1)
            start_lookup(0)
            for i in range(LOOKED):
                if i + 1 < LOOKED:
                    start_lookup(i + 1)
                else:
                    high_weights(0, FIRST_CHUNKS)
                if i == 0:
                    act.wait_ge(s_bank, 1)
                    nc.scalar.copy(embT[:, :, :, 0], pT[1][:, :].rearrange("d (t p) -> d t p", p=128)).then_inc(s_banka, 1)
                act.wait_ge(s_look, (i + 1) * VK)
                nc.scalar.copy(embT[:, :, :, 1 + i], pG[i % 2][:, 0, :].rearrange(
                    "d (t p) -> d t p", p=128)).then_inc(s_lookc, 1)
                if i > 0:
                    copy_bank(0, i - 1)
            for i in range(LOOKED - 1, len(BANKS)):
                copy_bank(0, i)
            act.wait_ge(s_banka, 1)
            nc.scalar.copy(bot_hi[:, :, :], embT[:, :, :, 0]).then_inc(s_bothi, 1)

            high_weights(FIRST_CHUNKS, KTILES + 1)

            for t in range(LAST):
                copy_gram(t, KTILES)
                high_products(t, 0, KTILES)
                copy_bank(t + 1, 0)
                copy_bank(t + 1, 1)
                if t == 0:
                    high_weights(KTILES + 1, CHUNKS)
                relu(t)
                for i in range(2, EARLY if t + 1 == LAST else len(BANKS)):
                    copy_bank(t + 1, i)
            copy_gram(LAST, LATE)
            high_products(LAST, 0, LATE)
            for i in range(EARLY, len(BANKS)):
                copy_bank(LAST, i)
            for h in range(2):
                act.wait_ge(s_gram, TILES + h + 1)
                gram_copies(nc.scalar.copy, late_blocks[:, h:h + 1, :, :], ROWS, h * BANK_GROUPS,
                            LATE, KTILES, (2, 3)).then_inc(s_ga, 1)
            act.wait_ge(s_gv, TILES + 2)
            act.wait_ge(s_ga, TILES + 2)
            nc.scalar.copy(prod_hi[:, LATE:KTILES, :], prod[:, LATE:KTILES, :]).then_inc(s_phi, 1)
            relu(LAST)

        @block.tensor
        def _(pe):
            def transpose_bank(t, i):
                slots = gathered_slots(BANKS[i])
                pe.wait_ge(s_row[t][i], 16 * len(slots))
                n = (t * len(BANKS) + i) // 2
                if not even(t, i):
                    pe.wait_ge(s_banka, 1 + n)
                elif n > 0:
                    pe.wait_ge(s_bankv, n)
                for m, g in enumerate(slots):
                    last = nc.tensor.transpose(bank(t, i)[:, m, :], emb[:, t % 2, g - LOOKED - 1, :], ident[:, :])
                last.then_inc(s_bank, 1)

            def banks_copied(t, n):
                total = t * len(BANKS) + n
                pe.wait_ge(s_bankv, (total + 1) // 2)
                pe.wait_ge(s_banka, 1 + total // 2)

            def gram(blocks, t, groups, rows, c0, c1):
                for i in groups:
                    for s in range(4):
                        p = 4 * i + s
                        last = nc.tensor.matmul(
                            blocks[32 * s:32 * s + rows, i // BANK_GROUPS, i % BANK_GROUPS, 0:c1 - c0],
                            embT[:, t, p, 0:rows], embT[:, t, p, c0:c1], start=True, stop=True)
                return last

            def terms(psum, a_hi, a_lo, b_hi, b_lo, start, stop, lo_ready):
                K = a_hi.shape[1]
                for k in range(K):
                    nc.tensor.matmul(psum, a_hi[:, k, :], b_hi[:, k, :], start=start and k == 0, stop=False)
                    nc.tensor.matmul(psum, a_hi[:, k, :], b_lo[:, k, :], start=False, stop=False)
                lo_ready()
                for k in range(K):
                    last = nc.tensor.matmul(psum, a_lo[:, k, :], b_hi[:, k, :], start=False, stop=stop and k == K - 1)
                return last

            def layer1(t, k1):
                if t == 0:
                    pe.wait_ge(s_wlo, KTILES + 1)
                    pe.wait_ge(s_bothi, 1)
                else:
                    pe.wait_ge(s_h1, t)
                terms(pH1[:, :], bot_hi[:, t:t + 1, :], bot_lo[:, t:t + 1, :], w1_hi[:, KTILES:, :],
                      w1_lo[:, KTILES:, :], True, False, lambda: pe.wait_ge(s_botlo, 1))
                pe.wait_ge(s_phi, t + 1)
                last = terms(pH1[:, :], prod_hi[:, 0:k1, :], prod_lo[:, 0:k1, :], w1_hi[:, 0:k1, :],
                             w1_lo[:, 0:k1, :], False, k1 == KTILES, lambda: pe.wait_ge(s_plo, t + 1))
                if k1 == KTILES:
                    last.then_inc(s_l1, 1)

            def transpose_h1(t):
                pe.wait_ge(s_h1, t + 1)
                for n in range(K2):
                    last = nc.tensor.transpose(pG[t % 2][:, 0, 128 * n:128 * (n + 1)],
                                               h1[:, 128 * n:128 * (n + 1)], ident[:, :])
                last.then_inc(s_h1p, 1)

            def layer2(t):
                if t == 0:
                    pe.wait_ge(s_wlo, CHUNKS)
                    pe.wait_ge(s_small, 32)
                    pe.wait_ge(s_ones, 1)
                else:
                    pe.wait_ge(s_y, t)
                nc.tensor.matmul(pH2[:, :], ones[0:1, :], b2s[:, :], start=True, stop=False)
                pe.wait_ge(s_h1hi, t + 1)
                terms(pH2[:, :], h1T_hi, h1T_lo, w2_hi, w2_lo, False, True,
                      lambda: pe.wait_ge(s_h1lo, t + 1)).then_inc(s_l2, 1)

            for i in range(LOOKED):
                if i >= 2:
                    pe.wait_ge(s_lookc, i - 1)
                pe.wait_ge(s_tabhi, i + 1)
                for k in range(VK):
                    if k < dve_tiles(i):
                        pe.wait_ge(s_hotv, i * VK - act_tiles_before(i) + k + 1)
                    else:
                        pe.wait_ge(s_hota, act_tiles_before(i) + k - dve_tiles(i) + 1)
                    nc.tensor.matmul(pG[i % 2][:, 0, :], tab_hi[:, i % 2, k, :], hot_rows(i, k),
                                     start=(k == 0), stop=False)
                pe.wait_ge(s_tablo, i + 1)
                for k in range(VK):
                    nc.tensor.matmul(pG[i % 2][:, 0, :], tab_lo[:, i % 2, k, :], hot_rows(i, k),
                                     start=False, stop=(k == VK - 1)).then_inc(s_look, 1)
                if i == 0:
                    pe.wait_ge(s_ident, 1)
                    pe.wait_ge(s_bot, 16)
                    for t in range(TILES):
                        last = nc.tensor.transpose(pT[1][:, 128 * t:128 * (t + 1)], bot[:, t, :], ident[:, :])
                    last.then_inc(s_bank, 1)
                else:
                    transpose_bank(0, i - 1)
            for i in range(LOOKED - 1, len(BANKS)):
                transpose_bank(0, i)

            pe.wait_ge(s_lookc, LOOKED)
            for t in range(LAST):
                banks_copied(t, len(BANKS))
                gram(gram_blocks(t), t, range(BANK_GROUPS), ROWS, 1, FEATURES)
                if t > 0:
                    transpose_h1(t - 1)
                gram(gram_blocks(t), t, range(BANK_GROUPS, GROUPS), ROWS, 1, FEATURES).then_inc(s_gram, 1)
                transpose_bank(t + 1, 0)
                transpose_bank(t + 1, 1)
                if t > 0:
                    layer2(t - 1)
                layer1(t, KTILES)
                for i in range(2, EARLY if t + 1 == LAST else len(BANKS)):
                    transpose_bank(t + 1, i)
            banks_copied(LAST, EARLY)
            gram(gram_blocks(LAST), LAST, range(BANK_GROUPS), 1 + 4 * LATE, 1, 1 + 4 * LATE)
            transpose_h1(LAST - 1)
            gram(gram_blocks(LAST), LAST, range(BANK_GROUPS, GROUPS), 1 + 4 * LATE, 1, 1 + 4 * LATE).then_inc(s_gram, 1)
            for i in range(EARLY, len(BANKS)):
                transpose_bank(LAST, i)
            layer2(LAST - 1)
            banks_copied(LAST, len(BANKS))
            for h in range(2):
                gram(late_blocks, LAST, range(h * BANK_GROUPS, (h + 1) * BANK_GROUPS), ROWS,
                     1 + 4 * LATE, FEATURES).then_inc(s_gram, 1)
            layer1(LAST, LATE)
            pe.wait_ge(s_phi, TILES + 1)
            terms(pH1[:, :], prod_hi[:, LATE:, :], prod_lo[:, LATE:, :], w1_hi[:, LATE:KTILES, :],
                  w1_lo[:, LATE:KTILES, :], False, True,
                  lambda: pe.wait_ge(s_plo, TILES + 1)).then_inc(s_l1, 1)
            transpose_h1(LAST)
            layer2(LAST)


def weight_rows():
    import numpy as np
    zero = FEATURES * (FEATURES - 1) // 2 + D + 1
    feature = [0] + [f + 1 for f in SLOT_TABLE[1:]]
    rows = np.full((4, 32, KTILES + 1), zero)
    for f in range(ROWS):
        for g in range(f + 1, FEATURES):
            k, j = divmod(g - 1, 4)
            a, b = sorted((feature[f], feature[g]))
            rows[j, f, k] = a * (2 * FEATURES - a - 1) // 2 + b - a - 1
    rows[0, BIAS_ROW, 0] = zero - 1
    rows = rows.reshape(128, KTILES + 1)
    rows[:, KTILES] = zero - 1 - D + np.arange(D)
    return rows


def kernel(**inputs):
    import numpy as np
    import concourse.bacc as bacc
    from concourse import mybir
    from concourse.bass_utils import run_bass_kernel_spmd as run

    nc = bacc.Bacc("TRN2", target_bir_lowering=False, num_devices=1)
    w1 = np.asarray(inputs["W_top1"])
    b1 = np.asarray(inputs["b_top1"])
    ids = np.asarray(inputs["ids"])
    arrays = {"bottom": inputs["r_bottom_output"], "ids": ids}
    arrays["hot_ids"] = ids.reshape(128, TILES, TABLES).transpose(2, 1, 0)[LOOKED_UP].reshape(LOOKED, B)
    arrays.update({f"tbl_{f}": inputs[f"tbl_{f}"] for f in range(TABLES)})
    arrays["w1"] = np.concatenate([w1, b1[None], np.zeros_like(b1[None])])[weight_rows()]
    arrays.update({"w2": inputs["W_top2"], "b2": inputs["b_top2"], "w3": inputs["W_top3"]})
    arrays = {name: np.ascontiguousarray(a) for name, a in arrays.items()}
    aps = {name: nc.dram_tensor(name, a.shape, mybir.dt.from_np(a.dtype), kind="ExternalInput").ap()
           for name, a in arrays.items()}
    out = nc.dram_tensor("out", (B, 1), mybir.dt.float32, kind="ExternalOutput").ap()
    tower(nc, aps["bottom"], aps["ids"], aps["hot_ids"], [aps[f"tbl_{f}"] for f in range(TABLES)],
          aps["w1"], aps["w2"], aps["b2"], aps["w3"], out)
    r = run(nc, [arrays], core_ids=[0])
    return r.results[0]["out"]
```

```python
import concourse.bass as bass
from concourse import mybir
from contextlib import ExitStack

B = 512
D = 128
TABLES = 26
FEATURES = TABLES + 1
TILES = B // 128
LAST = TILES - 1
GROUPS = 32
BANK_GROUPS = GROUPS // 2
ROWS = COLS = FEATURES - 1
KTILES = 4
FIRST = FEATURES - 4 * KTILES
MOVES = [
    (range(6, 10), 0, 9, 0, 23),
    (range(2, 6), 0, 5, 1, 26),
    (range(1, 11, 9), 0, 6, 2, 26),
    (range(10, 11), 6, 10, 3, 26)]
BIAS_QUADRANT, BIAS_ROW = 3, 31
H1_AFTER, L2_AFTER = 2, 4
N1, N2 = 512, 256
K2 = N1 // 128

LOOKED_UP = [3, 4, 5, 7, 8, 10, 20, 24, 25]
LOOKED = len(LOOKED_UP)
VOCAB = 1000
VP = 125
VK = VOCAB // VP
FIRST_CHUNKS = 2
RING = 3
HOT_RING = 14
CHUNKS = KTILES + 1 + 2
CHUNK_RING = 2 * RING
SLOT_TABLE = [None] + LOOKED_UP + [f for f in range(TABLES) if f not in LOOKED_UP]


def dve_tiles(i):
    return VK - 1 - i % 2


def act_tiles_before(i):
    return i * VK - sum(dve_tiles(j) for j in range(i))


def gathered_slots(k):
    return [g for g in range(FIRST + 4 * k, FIRST + 4 * k + 4) if g > LOOKED]


BANKS = [k for k in range(-2, KTILES) if gathered_slots(k)]


def tower(nc, bottom, ids, hot_ids, tables, w1, w2, b2, w3, out):
    fp32, fp32r, i32 = mybir.dt.float32, mybir.dt.float32r, mybir.dt.int32
    ALU, ACT = mybir.AluOpType, mybir.ActivationFunctionType

    ctx = ExitStack()
    with ctx:
        def sb(name, shape, dt=fp32):
            return ctx.enter_context(nc.sbuf_tensor(name, shape, dt))

        def pb(name, shape):
            return ctx.enter_context(nc.psum_tensor(name, shape, fp32))

        def sem(name):
            return ctx.enter_context(nc.semaphore(name))

        idx = sb("idx", [128, TILES * TABLES], i32)
        hot = sb("hot", [VP, RING, B], i32)
        row0 = sb("row0", [VP, 1], i32)
        row0f = sb("row0f", [VP, 1])
        minus_k = sb("minus_k", [VP, 2])
        tab = sb("tab", [128, RING, VK, D])
        tab_hi = sb("tab_hi", [VP, 2, VK, D], fp32r)
        tab_lo = sb("tab_lo", [VP, 2, VK, D], fp32r)
        square = sb("square", [VP, B])
        onehot = sb("onehot", [VP, HOT_RING, B], fp32r)
        bot = sb("bot", [128, TILES, D])
        emb = sb("emb", [128, 2, TABLES - LOOKED, D])
        embT = sb("embT", [128, TILES, 128, FEATURES])
        bot_hi = sb("bot_hi", [128, TILES, 128], fp32r)
        bot_lo = sb("bot_lo", [128, TILES, 128], fp32r)
        prod = sb("prod", [128, KTILES, 128])
        stage = sb("stage", [FIRST - 1, FIRST - 1, 128])
        prod_hi = sb("prod_hi", [128, KTILES, 128], fp32r)
        prod_lo = sb("prod_lo", [128, KTILES, 128], fp32r)
        w_hi = sb("w_hi", [128, CHUNKS, N1], fp32r)
        w_lo = sb("w_lo", [128, CHUNKS, N1], fp32r)
        b2s = sb("b2s", [1, N2])
        w3s = sb("w3s", [128, N2])
        ones = sb("ones", [128, 128])
        ident = sb("ident", [128, 128])
        h1 = sb("h1", [128, N1])
        h1T_hi = sb("h1T_hi", [128, K2, 128], fp32r)
        h1T_lo = sb("h1T_lo", [128, K2, 128], fp32r)
        h2w = sb("h2w", [128, N2])
        y = sb("y", [128, TILES])

        pT = [pb(f"pT{i}", [128, 512]) for i in range(2)]
        pG = [pb(f"pG{i}", [128, 2, 512]) for i in range(2)]
        pH1 = pb("pH1", [128, N1])
        pH2 = pb("pH2", [128, N2])

        s_ids = sem("s_ids")
        s_hotids = [sem(f"s_hotids{i}") for i in range(LOOKED)]
        s_tab = [sem(f"s_tab{i}") for i in range(LOOKED)]
        s_bot = sem("s_bot")
        s_w = [sem(f"s_w{c}") for c in range(CHUNKS)]
        s_small = sem("s_small")
        s_ident0 = sem("s_ident0")
        s_ident = sem("s_ident")
        s_row0 = sem("s_row0")
        s_row0f = sem("s_row0f")
        s_rel = sem("s_rel")
        s_ones = sem("s_ones")
        s_prod1 = sem("s_prod1")
        s_row = [[sem(f"s_row{t}_{k}") for k in BANKS] for t in range(TILES)]
        s_tabhi = sem("s_tabhi")
        s_tablo = sem("s_tablo")
        s_hotv = sem("s_hotv")
        s_sq = sem("s_sq")
        s_hota = sem("s_hota")
        s_look = sem("s_look")
        s_lookc = sem("s_lookc")
        s_bank = sem("s_bank")
        s_bankv = sem("s_bankv")
        s_banka = sem("s_banka")
        s_bothi = sem("s_bothi")
        s_botlo = sem("s_botlo")
        s_whi = sem("s_whi")
        s_wlo = sem("s_wlo")
        s_gram = sem("s_gram")
        s_gv = sem("s_gv")
        s_ga = sem("s_ga")
        s_stv = sem("s_stv")
        s_sta = sem("s_sta")
        s_moved = sem("s_moved")
        s_phi = sem("s_phi")
        s_plo = sem("s_plo")
        s_l1 = sem("s_l1")
        s_h1 = sem("s_h1")
        s_h1p = sem("s_h1p")
        s_h1hi = sem("s_h1hi")
        s_h1lo = sem("s_h1lo")
        s_l2 = sem("s_l2")
        s_y = sem("s_y")
        s_out = sem("s_out")

        block = ctx.enter_context(nc.Block())

        w1_hi, w1_lo = w_hi[:, 0:KTILES + 1, :], w_lo[:, 0:KTILES + 1, :]
        w2_hi, w2_lo = (w[:, KTILES + 1:, :].rearrange("p c (k n) -> p (c k) n", n=N2) for w in (w_hi, w_lo))

        def bank_slots(t, i):
            slots = gathered_slots(BANKS[i])
            return embT[:, t, :, slots[0]:slots[-1] + 1].rearrange("d p f -> d f p")

        def bank(t, i):
            return pT[(t * len(BANKS) + i) % 2][:, 0:128 * len(gathered_slots(BANKS[i]))].rearrange(
                "d (f p) -> d f p", p=128)

        def hot_rows(i, k):
            return onehot[:, (i * VK + k) % HOT_RING, :]

        def wait_hot_free(engine, i, k):
            if i * VK + k >= HOT_RING:
                engine.wait_ge(s_look, i * VK + k - HOT_RING + 1)

        def chunk(c):
            table = (LOOKED + (c % CHUNK_RING) // 2) % RING
            return tab[:, table, VK // 2 * (c % 2):VK // 2 * (c % 2 + 1), :].rearrange("p k d -> p (k d)")

        def even(t, i):
            return (t * len(BANKS) + i) % 2 == 0

        def gram_blocks(t):
            return pG[t % 2][:, :, 0:BANK_GROUPS * COLS].rearrange("p b (i c) -> p b i c", c=COLS)

        def copy_first(copy, blocks, quadrants):
            n = FIRST - 1
            for s in quadrants:
                last = copy(stage[:, :, s::4].rearrange("p k (b i) -> p b i k", b=2),
                            blocks[32 * s:32 * s + n, :, :, 0:n])
            return last

        def copy_columns(copy, blocks, quadrants):
            for s in quadrants:
                for j in range(4):
                    rows = FEATURES - 4 + j
                    last = copy(prod[32 * j:32 * j + rows, :, s::4].rearrange("p k (b i) -> p b i k", b=2),
                                blocks[32 * s:32 * s + rows, :, :, FIRST - 1 + j::4])
            return last

        @block.sync
        def _(sp):
            def load_lookup(i):
                if i >= RING:
                    sp.wait_ge(s_look, (i - RING + 1) * VK)
                sp.dma_start(hot[:, i % RING, :], hot_ids[i:i + 1, :].broadcast_to([VP, B])).then_inc(s_hotids[i], 16)
                sp.dma_start(tab[0:VP, i % RING, :, :], tables[LOOKED_UP[i]].rearrange(
                    "(p k) d -> p k d", k=VK)).then_inc(s_tab[i], 16)

            def load_weights(c):
                if c < CHUNK_RING:
                    sp.wait_ge(s_look, (LOOKED - RING + c // 2 + 1) * VK)
                else:
                    sp.wait_ge(s_wlo, c - CHUNK_RING + 1)
                if c <= KTILES:
                    dst, src = chunk(c), w1[:, c, :]
                else:
                    dst = chunk(c).rearrange("p (k n) -> p k n", n=N2)
                    src = w2.rearrange("(k p) n -> p k n", p=128)[:, 2 * (c - KTILES - 1):2 * (c - KTILES), :]
                sp.dma_start(dst, src).then_inc(s_w[c], 16)

            sp.dma_start(idx[:, :], ids.rearrange("(p t) f -> p (t f)", t=TILES)).then_inc(s_ids, 16)
            sp.dma_start(tab[0:VP, 0, :, :], tables[LOOKED_UP[0]].rearrange(
                "(p k) d -> p k d", k=VK)).then_inc(s_tab[0], 16)
            sp.dma_start(bot[:, :, :], bottom.rearrange("(p t) d -> p t d", t=TILES)).then_inc(s_bot, 16)
            load_lookup(1)
            load_lookup(2)
            sp.dma_start(b2s[:, :], b2.unsqueeze(0)).then_inc(s_small, 16)
            sp.dma_start(w3s[:, :], w3.rearrange("n o -> o n").broadcast_to([128, N2])).then_inc(s_small, 16)
            for i in range(RING, LOOKED):
                load_lookup(i)
            for c in range(CHUNKS):
                load_weights(c)
            for t in range(TILES):
                sp.wait_ge(s_stv, t + 1)
                sp.wait_ge(s_sta, t + 1)
                if t > 0:
                    sp.wait_ge(s_phi, t)
                    sp.wait_ge(s_plo, t)
                for columns, f0, f1, j, row in MOVES:
                    sp.dma_start(prod[32 * j + row:32 * j + row + f1 - f0, 0:len(columns), :],
                                 stage[f0:f1, columns[0] - 1:columns[-1]:columns.step, :]).then_inc(s_moved, 16)
            sp.wait_ge(s_y, TILES)
            sp.dma_start(out.rearrange("(p t) o -> p (t o)", t=TILES), y[:, :]).then_inc(s_out, 16)
            sp.wait_ge(s_out, 16)

        @block.gpsimd
        def _(pool):
            nc.gpsimd.iota(row0[:, :], [[0, 1]], base=0, channel_multiplier=VK).then_inc(s_row0, 1)
            nc.gpsimd.memset(ident[:, :], 0.0).then_inc(s_ident0, 1)
            pool.wait_ge(s_ident0, 1)
            nc.gpsimd.affine_select(out=ident[:, :], in_=ident[:, :], compare_op=ALU.not_equal, fill=1.0,
                                    base=0, pattern=[[-1, 128]], channel_multiplier=1).then_inc(s_ident, 1)
            pool.wait_ge(s_ids, 16)
            for t in range(TILES):
                for i, k in enumerate(BANKS):
                    if t >= 2:
                        pool.wait_ge(s_bank, 1 + (t - 2) * len(BANKS) + i + 1)
                    for g in gathered_slots(k):
                        f = SLOT_TABLE[g]
                        c = t * TABLES + f
                        nc.gpsimd.indirect_dma_start(
                            out=emb[:, t % 2, g - LOOKED - 1, :], out_offset=None, in_=tables[f],
                            in_offset=bass.IndirectOffsetOnAxis(ap=idx[:, c:c + 1], axis=0),
                        ).then_inc(s_row[t][i], 16)

        @block.vector
        def _(dve):
            def copy_bank(t, i):
                if even(t, i):
                    dve.wait_ge(s_bank, 1 + t * len(BANKS) + i + 1)
                    nc.vector.tensor_copy(bank_slots(t, i), bank(t, i)).then_inc(s_bankv, 1)

            def subtract(lo, whole, hi):
                return nc.vector.tensor_tensor(lo, whole, hi, ALU.subtract)

            def low_products(t):
                if t > 0:
                    dve.wait_ge(s_l1, t)
                dve.wait_ge(s_gv, t + 1)
                dve.wait_ge(s_phi, t + 1)
                subtract(prod_lo[:, :, :], prod[:, :, :], prod_hi[:, :, :]).then_inc(s_plo, 1)

            def copy_gram(t):
                dve.wait_ge(s_gram, t + 1)
                if t == 0:
                    dve.wait_ge(s_prod1, 1)
                else:
                    dve.wait_ge(s_phi, t)
                    dve.wait_ge(s_plo, t)
                    dve.wait_ge(s_moved, 16 * len(MOVES) * t)
                copy_first(nc.vector.tensor_copy, gram_blocks(t), (0, 1)).then_inc(s_stv, 1)
                copy_columns(nc.vector.tensor_copy, gram_blocks(t), (0, 1)).then_inc(s_gv, 1)

            def low_weights(c0, c1):
                for c in range(c0, c1):
                    dve.wait_ge(s_whi, c + 1)
                    subtract(w_lo[:, c, :], chunk(c), w_hi[:, c, :]).then_inc(s_wlo, 1)

            def split_h1(t):
                dve.wait_ge(s_h1p, t + 1)
                if t > 0:
                    dve.wait_ge(s_l2, t)
                whole = pG[t % 2][:, 0, :].rearrange("p (k b) -> p k b", b=128)
                nc.vector.tensor_copy(h1T_hi[:, :, :], whole).then_inc(s_h1hi, 1)
                dve.wait_ge(s_h1hi, t + 1)
                subtract(h1T_lo[:, :, :], whole, h1T_hi[:, :, :]).then_inc(s_h1lo, 1)

            def layer3(t):
                dve.wait_ge(s_l2, t + 1)
                if t == 0:
                    dve.wait_ge(s_small, 32)
                else:
                    dve.wait_ge(s_y, t)
                nc.vector.scalar_tensor_tensor(out=h2w[:, :], in0=pH2[:, :], scalar=0.0, in1=w3s[:, :],
                                               op0=ALU.max, op1=ALU.mult, accum_out=y[:, t:t + 1]).then_inc(s_y, 1)

            for m in range(2):
                nc.vector.memset(minus_k[:, m:m + 1], -float(VK - 2 + m))
            nc.vector.memset(ones[:, :], 1.0).then_inc(s_ones, 1)
            dve.wait_ge(s_row0, 1)
            nc.vector.tensor_copy(row0f[:, :], row0[:, :]).then_inc(s_row0f, 1)
            dve.wait_ge(s_row0f, 1)
            for i in range(LOOKED):
                dve.wait_ge(s_hotids[i], 16)
                nc.vector.tensor_scalar(hot[:, i % RING, :], hot[:, i % RING, :], row0f[:, :], None,
                                        ALU.subtract).then_inc(s_rel, 1)
                dve.wait_ge(s_rel, i + 1)
                for k in range(dve_tiles(i)):
                    wait_hot_free(dve, i, k)
                    nc.vector.tensor_scalar(hot_rows(i, k), hot[:, i % RING, :], float(k), None,
                                            ALU.is_equal).then_inc(s_hotv, 1)
                dve.wait_ge(s_tabhi, i + 1)
                if i >= 2:
                    dve.wait_ge(s_look, (i - 1) * VK)
                subtract(tab_lo[:, i % 2, :, :], tab[0:VP, i % RING, :, :], tab_hi[:, i % 2, :, :]).then_inc(s_tablo, 1)
                if 2 <= i < 2 + len(BANKS):
                    copy_bank(0, i - 2)
            low_weights(0, FIRST_CHUNKS)
            for i in range(LOOKED - 2, len(BANKS)):
                copy_bank(0, i)
            dve.wait_ge(s_bothi, 1)
            subtract(bot_lo[:, :, :], embT[:, :, :, 0], bot_hi[:, :, :]).then_inc(s_botlo, 1)

            low_weights(FIRST_CHUNKS, KTILES + 1)

            for i in range(0, len(BANKS)):
                copy_bank(1, i)
            for t in range(TILES):
                copy_gram(t)
                if t > 0:
                    for i in range(len(BANKS)):
                        if i == H1_AFTER:
                            split_h1(t - 1)
                        if t < LAST:
                            copy_bank(t + 1, i)
                else:
                    low_weights(KTILES + 1, CHUNKS)
                low_products(t)
                if t > 0:
                    layer3(t - 1)
            split_h1(LAST)
            layer3(LAST)

        @block.scalar
        def _(act):
            def copy_bank(t, i):
                if not even(t, i):
                    act.wait_ge(s_bank, 1 + t * len(BANKS) + i + 1)
                    nc.scalar.copy(bank_slots(t, i), bank(t, i)).then_inc(s_banka, 1)

            def start_lookup(i):
                act.wait_ge(s_tab[i], 16)
                if i >= 2:
                    act.wait_ge(s_look, (i - 1) * VK)
                nc.scalar.copy(tab_hi[:, i % 2, :, :], tab[0:VP, i % RING, :, :]).then_inc(s_tabhi, 1)
                act.wait_ge(s_rel, i + 1)
                for k in range(dve_tiles(i), VK):
                    n = act_tiles_before(i) + k - dve_tiles(i)
                    if n > 0:
                        act.wait_ge(s_hota, n)
                    nc.scalar.activation(square[:, :], hot[:, i % RING, :], ACT.Square,
                                         bias=minus_k[:, k - VK + 2:k - VK + 3]).then_inc(s_sq, 1)
                    act.wait_ge(s_sq, n + 1)
                    wait_hot_free(act, i, k)
                    nc.scalar.activation(hot_rows(i, k), square[:, :], ACT.Relu,
                                         bias=ones[0:VP, 0:1], scale=-1.0).then_inc(s_hota, 1)

            def high_weights(c0, c1):
                for c in range(c0, c1):
                    act.wait_ge(s_w[c], 16)
                    nc.scalar.copy(w_hi[:, c, :], chunk(c)).then_inc(s_whi, 1)

            def high_products(t):
                if t > 0:
                    act.wait_ge(s_l1, t)
                act.wait_ge(s_gv, t + 1)
                act.wait_ge(s_ga, t + 1)
                act.wait_ge(s_moved, 16 * len(MOVES) * (t + 1))
                nc.scalar.copy(prod_hi[:, :, :], prod[:, :, :]).then_inc(s_phi, 1)

            def copy_gram(t):
                act.wait_ge(s_gram, t + 1)
                if t == 0:
                    act.wait_ge(s_prod1, 1)
                else:
                    act.wait_ge(s_phi, t)
                    act.wait_ge(s_plo, t)
                    act.wait_ge(s_moved, 16 * len(MOVES) * t)
                copy_first(nc.scalar.copy, gram_blocks(t), (2, 3)).then_inc(s_sta, 1)
                copy_columns(nc.scalar.copy, gram_blocks(t), (2, 3)).then_inc(s_ga, 1)

            def relu(t):
                act.wait_ge(s_l1, t + 1)
                if t > 0:
                    act.wait_ge(s_h1p, t)
                nc.scalar.activation(h1[:, :], pH1[:, :], ACT.Relu).then_inc(s_h1, 1)

            act.dma_start(hot[:, 0, :], hot_ids[0:1, :].broadcast_to([VP, B])).then_inc(s_hotids[0], 16)
            act.wait_ge(s_ones, 1)
            nc.scalar.copy(prod[:, :, :], ones[:, :].unsqueeze(1).broadcast_to([128, KTILES, 128])).then_inc(s_prod1, 1)
            start_lookup(0)
            for i in range(LOOKED):
                if i + 1 < LOOKED:
                    start_lookup(i + 1)
                else:
                    high_weights(0, FIRST_CHUNKS)
                if i == 0:
                    act.wait_ge(s_bank, 1)
                    nc.scalar.copy(embT[:, :, :, 0], pT[1][:, :].rearrange("d (t p) -> d t p", p=128)).then_inc(s_banka, 1)
                act.wait_ge(s_look, (i + 1) * VK)
                nc.scalar.copy(embT[:, :, :, 1 + i], pG[i % 2][:, 0, :].rearrange(
                    "d (t p) -> d t p", p=128)).then_inc(s_lookc, 1)
                if 0 < i <= len(BANKS):
                    copy_bank(0, i - 1)
            act.wait_ge(s_banka, 1)
            nc.scalar.copy(bot_hi[:, :, :], embT[:, :, :, 0]).then_inc(s_bothi, 1)

            high_weights(FIRST_CHUNKS, KTILES + 1)

            for i in range(0, len(BANKS)):
                copy_bank(1, i)
            for t in range(TILES):
                copy_gram(t)
                if t > 0:
                    relu(t - 1)
                    if t < LAST:
                        for i in range(len(BANKS)):
                            copy_bank(t + 1, i)
                else:
                    high_weights(KTILES + 1, CHUNKS)
                high_products(t)
            relu(LAST)

        @block.tensor
        def _(pe):
            def transpose_bank(t, i):
                slots = gathered_slots(BANKS[i])
                pe.wait_ge(s_row[t][i], 16 * len(slots))
                n = (t * len(BANKS) + i) // 2
                if not even(t, i):
                    pe.wait_ge(s_banka, 1 + n)
                elif n > 0:
                    pe.wait_ge(s_bankv, n)
                for m, g in enumerate(slots):
                    last = nc.tensor.transpose(bank(t, i)[:, m, :], emb[:, t % 2, g - LOOKED - 1, :], ident[:, :])
                last.then_inc(s_bank, 1)

            def banks_copied(t, n):
                total = t * len(BANKS) + n
                pe.wait_ge(s_bankv, (total + 1) // 2)
                pe.wait_ge(s_banka, 1 + total // 2)

            def gram(t, groups):
                for i in groups:
                    for s in range(4):
                        p = 4 * i + s
                        last = nc.tensor.matmul(
                            gram_blocks(t)[32 * s:32 * s + ROWS, i // BANK_GROUPS, i % BANK_GROUPS, :],
                            embT[:, t, p, 0:ROWS], embT[:, t, p, 1:FEATURES], start=True, stop=True)
                    if i == GROUPS - 1:
                        last.then_inc(s_gram, 1)

            def terms(psum, a_hi, a_lo, b_hi, b_lo, start, stop, lo_ready):
                K = a_lo.shape[1]
                for k in range(K):
                    nc.tensor.matmul(psum, a_hi[:, k, :], b_hi[:, k, :], start=start and k == 0, stop=False)
                    nc.tensor.matmul(psum, a_hi[:, k, :], b_lo[:, k, :], start=False, stop=False)
                lo_ready()
                for k in range(K):
                    last = nc.tensor.matmul(psum, a_lo[:, k, :], b_hi[:, k, :], start=False, stop=stop and k == K - 1)
                return last

            def layer1(t):
                if t == 0:
                    pe.wait_ge(s_wlo, KTILES + 1)
                    pe.wait_ge(s_bothi, 1)
                else:
                    pe.wait_ge(s_h1, t)
                terms(pH1[:, :], bot_hi[:, t:t + 1, :], bot_lo[:, t:t + 1, :], w1_hi[:, KTILES:, :],
                      w1_lo[:, KTILES:, :], True, False, lambda: pe.wait_ge(s_botlo, 1))
                pe.wait_ge(s_phi, t + 1)
                terms(pH1[:, :], prod_hi, prod_lo, w1_hi, w1_lo, False, True,
                      lambda: pe.wait_ge(s_plo, t + 1)).then_inc(s_l1, 1)

            def transpose_h1(t):
                pe.wait_ge(s_h1, t + 1)
                for n in range(K2):
                    last = nc.tensor.transpose(pG[t % 2][:, 0, 128 * n:128 * (n + 1)],
                                               h1[:, 128 * n:128 * (n + 1)], ident[:, :])
                last.then_inc(s_h1p, 1)

            def layer2(t):
                if t == 0:
                    pe.wait_ge(s_wlo, CHUNKS)
                    pe.wait_ge(s_small, 32)
                    pe.wait_ge(s_ones, 1)
                else:
                    pe.wait_ge(s_y, t)
                nc.tensor.matmul(pH2[:, :], ones[0:1, :], b2s[:, :], start=True, stop=False)
                pe.wait_ge(s_h1hi, t + 1)
                terms(pH2[:, :], h1T_hi, h1T_lo, w2_hi, w2_lo, False, True,
                      lambda: pe.wait_ge(s_h1lo, t + 1)).then_inc(s_l2, 1)

            for i in range(LOOKED):
                if i >= 2:
                    pe.wait_ge(s_lookc, i - 1)
                pe.wait_ge(s_tabhi, i + 1)
                for k in range(VK):
                    if k < dve_tiles(i):
                        pe.wait_ge(s_hotv, i * VK - act_tiles_before(i) + k + 1)
                    else:
                        pe.wait_ge(s_hota, act_tiles_before(i) + k - dve_tiles(i) + 1)
                    nc.tensor.matmul(pG[i % 2][:, 0, :], tab_hi[:, i % 2, k, :], hot_rows(i, k),
                                     start=(k == 0), stop=False)
                pe.wait_ge(s_tablo, i + 1)
                for k in range(VK):
                    nc.tensor.matmul(pG[i % 2][:, 0, :], tab_lo[:, i % 2, k, :], hot_rows(i, k),
                                     start=False, stop=(k == VK - 1)).then_inc(s_look, 1)
                if i == 0:
                    pe.wait_ge(s_ident, 1)
                    pe.wait_ge(s_bot, 16)
                    for t in range(TILES):
                        last = nc.tensor.transpose(pT[1][:, 128 * t:128 * (t + 1)], bot[:, t, :], ident[:, :])
                    last.then_inc(s_bank, 1)
                elif i <= len(BANKS):
                    transpose_bank(0, i - 1)

            pe.wait_ge(s_lookc, LOOKED)
            for t in range(TILES):
                banks_copied(t, len(BANKS))
                if t == 0:
                    share = -(-GROUPS // len(BANKS))
                    for i in range(len(BANKS)):
                        gram(0, range(share * i, min(share * (i + 1), GROUPS)))
                        transpose_bank(1, i)
                else:
                    gram(t, range(GROUPS))
                    layer1(t - 1)
                    for i in range(len(BANKS)):
                        if i == H1_AFTER:
                            transpose_h1(t - 1)
                        if i == L2_AFTER:
                            layer2(t - 1)
                        if t < LAST:
                            transpose_bank(t + 1, i)
            layer1(LAST)
            transpose_h1(LAST)
            layer2(LAST)


def weight_rows():
    import numpy as np
    zero = FEATURES * (FEATURES - 1) // 2 + D + 1
    feature = [0] + [f + 1 for f in SLOT_TABLE[1:]]
    rows = np.full((4, 32, KTILES + 1), zero)
    place = {(f, g): ((g - FIRST) % 4, f, (g - FIRST) // 4) for g in range(FIRST, FEATURES) for f in range(g)}
    for columns, f0, f1, j, row in MOVES:
        place.update({(f, g): (j, row + f - f0, k) for k, g in enumerate(columns) for f in range(f0, min(f1, g))})
    for (f, g), at in place.items():
        a, b = sorted((feature[f], feature[g]))
        rows[at] = a * (2 * FEATURES - a - 1) // 2 + b - a - 1
    rows[BIAS_QUADRANT, BIAS_ROW, 0] = zero - 1
    rows = rows.reshape(128, KTILES + 1)
    rows[:, KTILES] = zero - 1 - D + np.arange(D)
    return rows


def kernel(**inputs):
    import numpy as np
    import concourse.bacc as bacc
    from concourse import mybir
    from concourse.bass_utils import run_bass_kernel_spmd as run

    nc = bacc.Bacc("TRN2", target_bir_lowering=False, num_devices=1)
    w1 = np.asarray(inputs["W_top1"])
    b1 = np.asarray(inputs["b_top1"])
    ids = np.asarray(inputs["ids"])
    arrays = {"bottom": inputs["r_bottom_output"], "ids": ids}
    arrays["hot_ids"] = ids.reshape(128, TILES, TABLES).transpose(2, 1, 0)[LOOKED_UP].reshape(LOOKED, B)
    arrays.update({f"tbl_{f}": inputs[f"tbl_{f}"] for f in range(TABLES)})
    arrays["w1"] = np.concatenate([w1, b1[None], np.zeros_like(b1[None])])[weight_rows()]
    arrays.update({"w2": inputs["W_top2"], "b2": inputs["b_top2"], "w3": inputs["W_top3"]})
    arrays = {name: np.ascontiguousarray(a) for name, a in arrays.items()}
    aps = {name: nc.dram_tensor(name, a.shape, mybir.dt.from_np(a.dtype), kind="ExternalInput").ap()
           for name, a in arrays.items()}
    out = nc.dram_tensor("out", (B, 1), mybir.dt.float32, kind="ExternalOutput").ap()
    tower(nc, aps["bottom"], aps["ids"], aps["hot_ids"], [aps[f"tbl_{f}"] for f in range(TABLES)],
          aps["w1"], aps["w2"], aps["b2"], aps["w3"], out)
    r = run(nc, [arrays], core_ids=[0])
    return r.results[0]["out"]
```

```python
import concourse.bass as bass
from concourse import mybir
from contextlib import ExitStack

B = 512
D = 128
TABLES = 26
FEATURES = TABLES + 1
TILES = B // 128
LAST = TILES - 1
GROUPS = 32
BANK_GROUPS = GROUPS // 2
ROWS = COLS = FEATURES - 1
KTILES = 4
FIRST = FEATURES - 4 * KTILES
MOVES = [
    (range(7, 11), 0, 10, 0, 14),
    (range(3, 7), 0, 6, 0, 24),
    (range(1, 3), 0, 2, 0, 30)]
WAIT_MOVES = 8
BIAS_QUADRANT, BIAS_ROW = 3, 31
N1, N2 = 512, 256
K2 = N1 // 128

LOOKED_UP = [3, 4, 5, 7, 8, 10, 20, 24, 25]
LOOKED = len(LOOKED_UP)
VOCAB = 1000
VP = 125
VP_MAIN = VP // 16 * 16
VK = VOCAB // VP
FIRST_CHUNKS = 2
RING = 3
HOT_RING = 14
CHUNKS = KTILES + 1 + 2
CHUNK_RING = 2 * RING
SLOT_TABLE = [None] + LOOKED_UP + [f for f in range(TABLES) if f not in LOOKED_UP]


def parts_through(t):
    return t + 1 + sum(halved <= t for halved in (LAST - 1, LAST))


def dve_tiles(i):
    return VK - 1 - i % 2


def act_tiles_before(i):
    return i * VK - sum(dve_tiles(j) for j in range(i))


BANKS = [range(g, min(g + 4, FEATURES)) for g in range(LOOKED + 1, FEATURES, 4)]


def tower(nc, bottom, ids, hot_ids, tables, w1, w2, b2, w3, out):
    fp32, fp32r, i32 = mybir.dt.float32, mybir.dt.float32r, mybir.dt.int32
    ALU, ACT = mybir.AluOpType, mybir.ActivationFunctionType

    ctx = ExitStack()
    with ctx:
        def sb(name, shape, dt=fp32):
            return ctx.enter_context(nc.sbuf_tensor(name, shape, dt))

        def pb(name, shape):
            return ctx.enter_context(nc.psum_tensor(name, shape, fp32))

        def sem(name):
            return ctx.enter_context(nc.semaphore(name))

        idx = sb("idx", [128, TILES * TABLES], i32)
        hot = sb("hot", [128, RING, B], i32)
        row0 = sb("row0", [VP, 1], i32)
        row0f = sb("row0f", [VP, 1])
        minus_k = sb("minus_k", [VP, 2])
        tab = sb("tab", [128, RING, VK, D])
        tab_hi = sb("tab_hi", [VP, 2, VK, D], fp32r)
        tab_lo = sb("tab_lo", [VP, 2, VK, D], fp32r)
        square = sb("square", [VP, B])
        onehot = sb("onehot", [VP, HOT_RING, B], fp32r)
        bot = sb("bot", [128, TILES, D])
        emb = sb("emb", [128, 2, TABLES - LOOKED, D])
        embT = sb("embT", [128, TILES, 128, FEATURES])
        bot_hi = sb("bot_hi", [128, TILES, 128], fp32r)
        bot_lo = sb("bot_lo", [128, TILES, 128], fp32r)
        prod = sb("prod", [128, KTILES, 128])
        stage = sb("stage", [FIRST - 1, FIRST - 1, 128])
        prod_hi = sb("prod_hi", [128, KTILES, 128], fp32r)
        prod_lo = sb("prod_lo", [128, KTILES, 128], fp32r)
        w_hi = sb("w_hi", [128, CHUNKS, N1], fp32r)
        w_lo = sb("w_lo", [128, CHUNKS, N1], fp32r)
        b2s = sb("b2s", [1, N2])
        w3s = sb("w3s", [128, N2])
        b2_hi = sb("b2_hi", [1, N2], fp32r)
        b2_lo = sb("b2_lo", [1, N2], fp32r)
        ones = sb("ones", [128, 128])
        ones_r = sb("ones_r", [1, 128], fp32r)
        ident = sb("ident", [128, 128])
        h1 = sb("h1", [128, N1])
        h1T_hi = sb("h1T_hi", [128, K2, 128], fp32r)
        h1T_lo = sb("h1T_lo", [128, K2, 128], fp32r)
        h2w = sb("h2w", [128, N2])
        y = sb("y", [128, TILES])

        pT = [pb(f"pT{i}", [128, 512]) for i in range(2)]
        pG = [pb(f"pG{i}", [128, 2, 512]) for i in range(2)]
        pH1 = pb("pH1", [128, N1])
        pH2 = pb("pH2", [128, N2])

        s_ids = sem("s_ids")
        s_hotids = [sem(f"s_hotids{i}") for i in range(LOOKED)]
        s_tab = [sem(f"s_tab{i}") for i in range(LOOKED)]
        s_tab0_rest = sem("s_tab0_rest")
        s_bot = sem("s_bot")
        s_w = [sem(f"s_w{c}") for c in range(CHUNKS)]
        s_small = sem("s_small")
        s_b2 = sem("s_b2")
        s_ident0 = sem("s_ident0")
        s_ident = sem("s_ident")
        s_row0 = sem("s_row0")
        s_row0f = sem("s_row0f")
        s_rel = sem("s_rel")
        s_ones = sem("s_ones")
        s_prod1 = sem("s_prod1")
        s_row = [[sem(f"s_row{t}_{k}") for k in range(len(BANKS))] for t in range(TILES)]
        s_tabhi = sem("s_tabhi")
        s_tablo = sem("s_tablo")
        s_hotv = sem("s_hotv")
        s_sq = sem("s_sq")
        s_hota = sem("s_hota")
        s_look = sem("s_look")
        s_lookc = sem("s_lookc")
        s_bank = sem("s_bank")
        s_bankv = sem("s_bankv")
        s_banka = sem("s_banka")
        s_bothi = sem("s_bothi")
        s_botlo = sem("s_botlo")
        s_whi = sem("s_whi")
        s_wlo = sem("s_wlo")
        s_gram = sem("s_gram")
        s_gv = sem("s_gv")
        s_ga = sem("s_ga")
        s_stv = sem("s_stv")
        s_sta = sem("s_sta")
        s_moved = sem("s_moved")
        s_movedp = sem("s_movedp")
        s_phi = sem("s_phi")
        s_plo = sem("s_plo")
        s_l1 = sem("s_l1")
        s_h1 = sem("s_h1")
        s_h1p = sem("s_h1p")
        s_h1hi = sem("s_h1hi")
        s_h1lo = sem("s_h1lo")
        s_l2 = sem("s_l2")
        s_y = sem("s_y")
        s_out = sem("s_out")

        block = ctx.enter_context(nc.Block())

        w1_hi, w1_lo = w_hi[:, 0:KTILES + 1, :], w_lo[:, 0:KTILES + 1, :]
        w2_hi, w2_lo = (w[:, KTILES + 1:, :].rearrange("p c (k n) -> p (c k) n", n=N2) for w in (w_hi, w_lo))

        def bank_slots(t, i):
            slots = BANKS[i]
            return embT[:, t, :, slots[0]:slots[-1] + 1].rearrange("d p f -> d f p")

        def bank(t, i):
            return pT[(t * len(BANKS) + i) % 2][:, 0:128 * len(BANKS[i])].rearrange(
                "d (f p) -> d f p", p=128)

        def hot_rows(i, k):
            return onehot[:, (i * VK + k) % HOT_RING, :]

        def wait_hot_free(engine, i, k):
            if i * VK + k >= HOT_RING:
                engine.wait_ge(s_look, i * VK + k - HOT_RING + 1)

        def chunk(c):
            table = (LOOKED + (c % CHUNK_RING) // 2) % RING
            return tab[:, table, VK // 2 * (c % 2):VK // 2 * (c % 2 + 1), :].rearrange("p k d -> p (k d)")

        def even(t, i):
            return (t * len(BANKS) + i) % 2 == 0

        def gram_blocks(t):
            return pG[t % 2][:, :, 0:BANK_GROUPS * COLS].rearrange("p b (i c) -> p b i c", c=COLS)

        def h1_turned(t, half):
            return pG[t % 2][:, half, 0:256].rearrange("p (k b) -> p k b", b=128)

        def first_columns(copy, t, halves, quadrants):
            for s in quadrants:
                last = copy(stage[:, :, 64 * halves[0] + s:64 * (halves[-1] + 1):4].rearrange(
                                "p k (b i) -> p b i k", i=BANK_GROUPS),
                            gram_blocks(t)[32 * s:32 * s + FIRST - 1, halves[0]:halves[-1] + 1, :, 0:FIRST - 1])
            return last

        def last_columns(copy, t, halves, quadrants):
            for s in quadrants:
                for j in range(4):
                    first = FIRST + 4 * j
                    rows = first + 3
                    last = copy(prod[32 * j:32 * j + rows, :, 64 * halves[0] + s:64 * (halves[-1] + 1):4].rearrange(
                                    "p k (b i) -> p b i k", i=BANK_GROUPS),
                                gram_blocks(t)[32 * s:32 * s + rows, halves[0]:halves[-1] + 1, :, first - 1:first + 3])
            return last

        def h1_parts(t):
            if t < LAST:
                return [(pH1[:, :], slice(0, N1))]
            return [(pH1[:, 0:N1 // 2], slice(0, N1 // 2)), (pT[1][:, 0:N1 // 2], slice(N1 // 2, N1))]

        def move(engine, moved, columns, f0, f1, j, row):
            engine.dma_start(prod[32 * j + row:32 * j + row + f1 - f0, 0:len(columns), :],
                             stage[f0:f1, columns[0] - 1:columns[-1], :]).then_inc(moved, 16)

        @block.sync
        def _(sp):
            def load_table(i, p0, p1, k0, k1, loaded):
                sp.dma_start(tab[p0:p1, i % RING, k0:k1, :], tables[LOOKED_UP[i]].rearrange(
                    "(p k) d -> p k d", k=VK)[p0:p1, k0:k1, :]).then_inc(loaded, 16)

            def load_lookup(i):
                if i >= RING:
                    sp.wait_ge(s_look, (i - RING + 1) * VK)
                sp.dma_start(hot[:, i % RING, :], hot_ids[i:i + 1, :].broadcast_to([128, B])).then_inc(s_hotids[i], 16)
                load_table(i, 0, VP_MAIN, 0, VK, s_tab[i])
                load_table(i, VP_MAIN, VP, 0, VK, s_tab[i])

            def load_weights(c):
                if c < CHUNK_RING:
                    sp.wait_ge(s_look, (LOOKED - RING + c // 2 + 1) * VK)
                else:
                    sp.wait_ge(s_wlo, c - CHUNK_RING + 1)
                if c <= KTILES:
                    dst, src = chunk(c), w1[:, c, :]
                else:
                    dst = chunk(c).rearrange("p (k n) -> p k n", n=N2)
                    src = w2.rearrange("(k p) n -> p k n", p=128)[:, 2 * (c - KTILES - 1):2 * (c - KTILES), :]
                sp.dma_start(dst, src).then_inc(s_w[c], 16)

            sp.dma_start(idx[:, :], ids.rearrange("(p t) f -> p (t f)", t=TILES)).then_inc(s_ids, 16)
            load_table(0, 0, VP_MAIN, 0, VK // 2, s_tab[0])
            load_table(0, VP_MAIN, VP, 0, VK, s_tab[0])
            load_table(0, 0, VP_MAIN, VK // 2, VK, s_tab0_rest)
            sp.dma_start(bot[:, :, :], bottom.rearrange("(p t) d -> p t d", t=TILES)).then_inc(s_bot, 16)
            load_lookup(1)
            load_lookup(2)
            sp.dma_start(b2s[:, :], b2.unsqueeze(0)).then_inc(s_small, 16)
            sp.dma_start(w3s[:, :], w3.rearrange("n o -> o n").broadcast_to([128, N2])).then_inc(s_small, 16)
            for i in range(RING, LOOKED):
                load_lookup(i)
            for c in range(CHUNKS):
                load_weights(c)
            for t in range(TILES):
                sp.wait_ge(s_stv, parts_through(t))
                sp.wait_ge(s_sta, parts_through(t))
                if t > 0:
                    sp.wait_ge(s_phi, t)
                    sp.wait_ge(s_plo, t)
                for step in MOVES if t < LAST else MOVES[1:]:
                    move(sp, s_moved, *step)
            sp.wait_ge(s_y, TILES)
            sp.dma_start(out.rearrange("(p t) o -> p (t o)", t=TILES), y[:, :]).then_inc(s_out, 16)
            sp.wait_ge(s_out, 16)

        @block.gpsimd
        def _(pool):
            nc.gpsimd.iota(row0[:, :], [[0, 1]], base=0, channel_multiplier=VK).then_inc(s_row0, 1)
            nc.gpsimd.memset(ident[:, :], 0.0).then_inc(s_ident0, 1)
            pool.wait_ge(s_ident0, 1)
            nc.gpsimd.affine_select(out=ident[:, :], in_=ident[:, :], compare_op=ALU.not_equal, fill=1.0,
                                    base=0, pattern=[[-1, 128]], channel_multiplier=1).then_inc(s_ident, 1)
            pool.wait_ge(s_ids, 16)
            for t in range(TILES):
                for i, slots in enumerate(BANKS):
                    if t >= 2:
                        pool.wait_ge(s_bank, 1 + (t - 2) * len(BANKS) + i + 1)
                    for g in slots:
                        f = SLOT_TABLE[g]
                        c = t * TABLES + f
                        nc.gpsimd.indirect_dma_start(
                            out=emb[:, t % 2, g - LOOKED - 1, :], out_offset=None, in_=tables[f],
                            in_offset=bass.IndirectOffsetOnAxis(ap=idx[:, c:c + 1], axis=0),
                        ).then_inc(s_row[t][i], 16)
            pool.wait_ge(s_stv, parts_through(LAST))
            pool.wait_ge(s_sta, parts_through(LAST))
            pool.wait_ge(s_phi, LAST)
            pool.wait_ge(s_plo, LAST)
            move(nc.gpsimd, s_movedp, *MOVES[0])

        @block.vector
        def _(dve):
            def copy_bank(t, i):
                if even(t, i):
                    dve.wait_ge(s_bank, 1 + t * len(BANKS) + i + 1)
                    nc.vector.tensor_copy(bank_slots(t, i), bank(t, i)).then_inc(s_bankv, 1)

            def subtract(lo, whole, hi):
                return nc.vector.tensor_tensor(lo, whole, hi, ALU.subtract)

            def low_products(t):
                if t > 0:
                    dve.wait_ge(s_l1, t)
                dve.wait_ge(s_gv, parts_through(t))
                dve.wait_ge(s_phi, t + 1)
                subtract(prod_lo[:, :, :], prod[:, :, :], prod_hi[:, :, :]).then_inc(s_plo, 1)

            def copy_stage(t, halves=(0, 1)):
                dve.wait_ge(s_gram, 2 * t + halves[-1] + 1)
                if t > 0:
                    dve.wait_ge(s_moved, 16 * len(MOVES) * t)
                first_columns(nc.vector.tensor_copy, t, halves, (0, 1)).then_inc(s_stv, 1)

            def copy_products(t, halves=(0, 1)):
                if t == 0:
                    dve.wait_ge(s_prod1, 1)
                else:
                    dve.wait_ge(s_phi, t)
                    dve.wait_ge(s_plo, t)
                last_columns(nc.vector.tensor_copy, t, halves, (0, 1)).then_inc(s_gv, 1)

            def low_weights(c0, c1):
                for c in range(c0, c1):
                    dve.wait_ge(s_whi, c + 1)
                    subtract(w_lo[:, c, :], chunk(c), w_hi[:, c, :]).then_inc(s_wlo, 1)

            def low_h1(t):
                for half in range(2):
                    dve.wait_ge(s_h1hi, 2 * t + half + 1)
                    if t > 0:
                        dve.wait_ge(s_l2, t)
                    subtract(h1T_lo[:, 2 * half:2 * half + 2, :], h1_turned(t, half),
                             h1T_hi[:, 2 * half:2 * half + 2, :]).then_inc(s_h1lo, 1)

            def layer3(t):
                dve.wait_ge(s_l2, t + 1)
                if t > 0:
                    dve.wait_ge(s_y, t)
                nc.vector.scalar_tensor_tensor(out=h2w[:, :], in0=pH2[:, :], scalar=0.0, in1=w3s[:, :],
                                               op0=ALU.max, op1=ALU.mult, accum_out=y[:, t:t + 1]).then_inc(s_y, 1)

            for m in range(2):
                nc.vector.memset(minus_k[:, m:m + 1], -float(VK - 2 + m))
            nc.vector.memset(ones[:, :], 1.0).then_inc(s_ones, 1)
            dve.wait_ge(s_row0, 1)
            nc.vector.tensor_copy(row0f[:, :], row0[:, :]).then_inc(s_row0f, 1)
            dve.wait_ge(s_row0f, 1)
            for i in range(LOOKED):
                dve.wait_ge(s_hotids[i], 16)
                nc.vector.tensor_scalar(hot[0:VP, i % RING, :], hot[0:VP, i % RING, :], row0f[:, :], None,
                                        ALU.subtract).then_inc(s_rel, 1)
                dve.wait_ge(s_rel, i + 1)
                for k in range(dve_tiles(i)):
                    wait_hot_free(dve, i, k)
                    nc.vector.tensor_scalar(hot_rows(i, k), hot[0:VP, i % RING, :], float(k), None,
                                            ALU.is_equal).then_inc(s_hotv, 1)
                dve.wait_ge(s_tabhi, i + 2)
                if i >= 2:
                    dve.wait_ge(s_look, (i - 1) * VK)
                subtract(tab_lo[:, i % 2, :, :], tab[0:VP, i % RING, :, :], tab_hi[:, i % 2, :, :]).then_inc(s_tablo, 1)
                if 2 <= i < 2 + len(BANKS):
                    copy_bank(0, i - 2)
            low_weights(0, FIRST_CHUNKS)
            dve.wait_ge(s_bothi, 1)
            subtract(bot_lo[:, :, :], embT[:, :, :, 0], bot_hi[:, :, :]).then_inc(s_botlo, 1)

            dve.wait_ge(s_small, 32)
            nc.vector.tensor_copy(ones_r[:, :], ones[0:1, :]).then_inc(s_b2, 1)
            nc.vector.tensor_copy(b2_hi[:, :], b2s[:, :]).then_inc(s_b2, 1)
            dve.wait_ge(s_b2, 2)
            subtract(b2_lo[:, :], b2s[:, :], b2_hi[:, :]).then_inc(s_b2, 1)

            copy_bank(1, 0)
            copy_bank(1, 1)
            low_weights(FIRST_CHUNKS, 3)
            copy_bank(1, 2)
            copy_bank(1, 3)
            low_weights(3, 4)
            copy_bank(1, 4)
            low_weights(4, KTILES + 1)

            copy_stage(0)
            copy_bank(2, 0)
            copy_bank(2, 1)
            copy_products(0)
            low_products(0)

            copy_stage(1)
            low_weights(KTILES + 1, CHUNKS)
            copy_products(1)
            copy_bank(2, 2)
            low_h1(0)
            copy_bank(2, 3)
            copy_bank(2, 4)
            low_products(1)
            layer3(0)

            copy_stage(2, [0])
            copy_products(2, [0])
            copy_stage(2, [1])
            copy_products(2, [1])
            copy_bank(3, 0)
            copy_bank(3, 1)
            low_h1(1)
            low_products(2)
            copy_bank(3, 2)
            layer3(1)
            copy_bank(3, 3)
            copy_bank(3, 4)
            low_h1(2)

            copy_stage(3, [0])
            copy_products(3, [0])
            copy_stage(3, [1])
            copy_products(3, [1])
            layer3(2)
            low_products(3)
            low_h1(3)
            layer3(3)

        @block.scalar
        def _(act):
            def copy_bank(t, i):
                if not even(t, i):
                    act.wait_ge(s_bank, 1 + t * len(BANKS) + i + 1)
                    nc.scalar.copy(bank_slots(t, i), bank(t, i)).then_inc(s_banka, 1)

            def start_lookup(i):
                if i >= 2:
                    act.wait_ge(s_look, (i - 1) * VK)
                step = VK // 2 if i == 0 else VK
                for k in range(0, VK, step):
                    if k == 0:
                        act.wait_ge(s_tab[i], 32)
                    else:
                        act.wait_ge(s_tab0_rest, 16)
                    nc.scalar.copy(tab_hi[:, i % 2, k:k + step, :], tab[0:VP, i % RING, k:k + step, :]).then_inc(s_tabhi, 1)
                act.wait_ge(s_rel, i + 1)
                for k in range(dve_tiles(i), VK):
                    n = act_tiles_before(i) + k - dve_tiles(i)
                    if n > 0:
                        act.wait_ge(s_hota, n)
                    nc.scalar.activation(square[:, :], hot[0:VP, i % RING, :], ACT.Square,
                                         bias=minus_k[:, k - VK + 2:k - VK + 3]).then_inc(s_sq, 1)
                    act.wait_ge(s_sq, n + 1)
                    wait_hot_free(act, i, k)
                    nc.scalar.activation(hot_rows(i, k), square[:, :], ACT.Relu,
                                         bias=ones[0:VP, 0:1], scale=-1.0).then_inc(s_hota, 1)

            def high_weights(c0, c1):
                for c in range(c0, c1):
                    act.wait_ge(s_w[c], 16)
                    nc.scalar.copy(w_hi[:, c, :], chunk(c)).then_inc(s_whi, 1)

            def high_products(t):
                if t > 0:
                    act.wait_ge(s_l1, t)
                act.wait_ge(s_gv, parts_through(t))
                act.wait_ge(s_ga, parts_through(t))
                act.wait_ge(s_moved, 16 * (len(MOVES) * (t + 1) - (t == LAST)))
                if t == LAST:
                    act.wait_ge(s_movedp, 16)
                nc.scalar.copy(prod_hi[:, :, :], prod[:, :, :]).then_inc(s_phi, 1)

            def copy_stage(t, halves=(0, 1)):
                act.wait_ge(s_gram, 2 * t + halves[-1] + 1)
                if t > 0:
                    act.wait_ge(s_moved, 16 * len(MOVES) * t)
                first_columns(nc.scalar.copy, t, halves, (2, 3)).then_inc(s_sta, 1)

            def copy_products(t, halves=(0, 1)):
                if t == 0:
                    act.wait_ge(s_prod1, 1)
                else:
                    act.wait_ge(s_phi, t)
                    act.wait_ge(s_plo, t)
                last_columns(nc.scalar.copy, t, halves, (2, 3)).then_inc(s_ga, 1)

            def relu(t, halves=(0, 1)):
                for half in halves:
                    act.wait_ge(s_l1, t + 1 if t < LAST else t + 1 + half)
                    if t > 0:
                        act.wait_ge(s_h1p, 2 * (t - 1) + half + 1)
                    cols = slice(N1 // 2 * half, N1 // 2 * (half + 1))
                    psum = pH1[:, cols] if t < LAST else h1_parts(t)[half][0]
                    nc.scalar.activation(h1[:, cols], psum, ACT.Relu).then_inc(s_h1, 1)

            def high_h1(t, halves=(0, 1)):
                for half in halves:
                    act.wait_ge(s_h1p, 2 * t + half + 1)
                    if t > 0:
                        act.wait_ge(s_l2, t)
                    nc.scalar.copy(h1T_hi[:, 2 * half:2 * half + 2, :], h1_turned(t, half)).then_inc(s_h1hi, 1)

            act.dma_start(hot[:, 0, :], hot_ids[0:1, :].broadcast_to([128, B])).then_inc(s_hotids[0], 16)
            act.wait_ge(s_ones, 1)
            nc.scalar.copy(prod[:, :, :], ones[:, :].unsqueeze(1).broadcast_to([128, KTILES, 128])).then_inc(s_prod1, 1)
            start_lookup(0)
            for i in range(LOOKED):
                if i + 1 < LOOKED:
                    start_lookup(i + 1)
                else:
                    high_weights(0, FIRST_CHUNKS)
                if i == 0:
                    act.wait_ge(s_bank, 1)
                    nc.scalar.copy(embT[:, :, :, 0], pT[1][:, :].rearrange("d (t p) -> d t p", p=128)).then_inc(s_banka, 1)
                act.wait_ge(s_look, (i + 1) * VK)
                nc.scalar.copy(embT[:, :, :, 1 + i], pG[i % 2][:, 0, :].rearrange(
                    "d (t p) -> d t p", p=128)).then_inc(s_lookc, 1)
                if 0 < i <= len(BANKS):
                    copy_bank(0, i - 1)
            act.wait_ge(s_banka, 1)
            nc.scalar.copy(bot_hi[:, :, :], embT[:, :, :, 0]).then_inc(s_bothi, 1)

            copy_bank(1, 0)
            copy_bank(1, 1)
            high_weights(FIRST_CHUNKS, 3)
            copy_bank(1, 2)
            copy_bank(1, 3)
            high_weights(3, 4)
            copy_bank(1, 4)
            high_weights(4, KTILES + 1)

            copy_stage(0)
            copy_bank(2, 0)
            copy_bank(2, 1)
            copy_products(0)
            high_products(0)

            copy_stage(1)
            high_weights(KTILES + 1, CHUNKS)
            copy_products(1)
            relu(0)
            copy_bank(2, 2)
            high_h1(0)
            copy_bank(2, 3)
            high_products(1)
            copy_bank(2, 4)

            copy_stage(2, [0])
            copy_products(2, [0])
            copy_stage(2, [1])
            copy_products(2, [1])
            relu(1)
            copy_bank(3, 0)
            copy_bank(3, 1)
            high_h1(1)
            high_products(2)
            copy_bank(3, 2)
            copy_bank(3, 3)
            relu(2)
            copy_bank(3, 4)
            high_h1(2)

            copy_stage(3, [0])
            copy_products(3, [0])
            copy_stage(3, [1])
            copy_products(3, [1])
            high_products(3)
            for half in range(2):
                relu(3, [half])
                high_h1(3, [half])

        @block.tensor
        def _(pe):
            def transpose_bank(t, i):
                slots = BANKS[i]
                pe.wait_ge(s_row[t][i], 16 * len(slots))
                n = (t * len(BANKS) + i) // 2
                if not even(t, i):
                    pe.wait_ge(s_banka, 1 + n)
                elif n > 0:
                    pe.wait_ge(s_bankv, n)
                for m, g in enumerate(slots):
                    last = nc.tensor.transpose(bank(t, i)[:, m, :], emb[:, t % 2, g - LOOKED - 1, :], ident[:, :])
                last.then_inc(s_bank, 1)

            def gram(t, half):
                if half == 0:
                    copied = (t + 1) * len(BANKS)
                    pe.wait_ge(s_bankv, (copied + 1) // 2)
                    pe.wait_ge(s_banka, 1 + copied // 2)
                for i in range(BANK_GROUPS):
                    for s in range(4):
                        p = 4 * (half * BANK_GROUPS + i) + s
                        last = nc.tensor.matmul(gram_blocks(t)[32 * s:32 * s + ROWS, half, i, :],
                                                embT[:, t, p, 0:ROWS], embT[:, t, p, 1:FEATURES], start=True, stop=True)
                last.then_inc(s_gram, 1)

            def high_terms(psum, a_hi, b_hi, b_lo, start, ready):
                for k in range(b_hi.shape[1]):
                    ready(k)
                    nc.tensor.matmul(psum, a_hi[:, k, :], b_hi[:, k, :], start=start and k == 0, stop=False)
                    nc.tensor.matmul(psum, a_hi[:, k, :], b_lo[:, k, :], start=False, stop=False)

            def low_terms(psum, a_lo, b_hi, stop, ready):
                K = b_hi.shape[1]
                for k in range(K):
                    ready(k)
                    last = nc.tensor.matmul(psum, a_lo[:, k, :], b_hi[:, k, :], start=False, stop=stop and k == K - 1)
                return last

            def layer1_bottom(t):
                if t == 0:
                    pe.wait_ge(s_wlo, KTILES + 1)
                    pe.wait_ge(s_bothi, 1)
                    pe.wait_ge(s_botlo, 1)
                else:
                    pe.wait_ge(s_h1, 2 * t)
                for psum, cols in h1_parts(t):
                    high_terms(psum, bot_hi[:, t:t + 1, :], w1_hi[:, KTILES:, cols], w1_lo[:, KTILES:, cols], True,
                               lambda k: None)
                    low_terms(psum, bot_lo[:, t:t + 1, :], w1_hi[:, KTILES:, cols], False, lambda k: None)

            def layer1_high(t, part):
                psum, cols = part
                high_terms(psum, prod_hi, w1_hi[:, 0:KTILES, cols], w1_lo[:, 0:KTILES, cols], False,
                           lambda k: pe.wait_ge(s_phi, t + 1))

            def layer1_low(t, part):
                psum, cols = part
                low_terms(psum, prod_lo, w1_hi[:, 0:KTILES, cols], True,
                          lambda k: pe.wait_ge(s_plo, t + 1)).then_inc(s_l1, 1)

            def layer1_products(t):
                for part in h1_parts(t):
                    layer1_high(t, part)
                    layer1_low(t, part)

            def transpose_h1(t, halves=(0, 1)):
                for half in halves:
                    pe.wait_ge(s_h1, 2 * t + half + 1)
                    for n in range(2):
                        col = 128 * (2 * half + n)
                        last = nc.tensor.transpose(h1_turned(t, half)[:, n, :], h1[:, col:col + 128], ident[:, :])
                    last.then_inc(s_h1p, 1)

            def layer2_high(t, half):
                if half == 0:
                    if t == 0:
                        pe.wait_ge(s_wlo, CHUNKS)
                        pe.wait_ge(s_b2, 3)
                    else:
                        pe.wait_ge(s_y, t)
                    nc.tensor.matmul(pH2[:, :], ones_r[:, :], b2_hi[:, :], start=True, stop=False)
                    nc.tensor.matmul(pH2[:, :], ones_r[:, :], b2_lo[:, :], start=False, stop=False)
                tiles = slice(2 * half, 2 * half + 2)
                high_terms(pH2[:, :], h1T_hi[:, tiles, :], w2_hi[:, tiles, :], w2_lo[:, tiles, :], False,
                           lambda k: pe.wait_ge(s_h1hi, 2 * t + half + 1))

            def layer2_low(t, half):
                tiles = slice(2 * half, 2 * half + 2)
                last = low_terms(pH2[:, :], h1T_lo[:, tiles, :], w2_hi[:, tiles, :], half == 1,
                                 lambda k: pe.wait_ge(s_h1lo, 2 * t + half + 1))
                if half == 1:
                    last.then_inc(s_l2, 1)

            def layer2(t):
                for half in range(2):
                    layer2_high(t, half)
                for half in range(2):
                    layer2_low(t, half)

            def stay_busy(n):
                for _ in range(n):
                    nc.tensor.matmul(pT[0][:, :], w1_hi[:, 0, 0:128], w1_hi[:, 0, :], start=True, stop=True)

            for i in range(LOOKED):
                if i >= 2:
                    pe.wait_ge(s_lookc, i - 1)
                for k in range(VK):
                    pe.wait_ge(s_tabhi, i + 1 if i == 0 and k < VK // 2 else i + 2)
                    if k < dve_tiles(i):
                        pe.wait_ge(s_hotv, i * VK - act_tiles_before(i) + k + 1)
                    else:
                        pe.wait_ge(s_hota, act_tiles_before(i) + k - dve_tiles(i) + 1)
                    nc.tensor.matmul(pG[i % 2][:, 0, :], tab_hi[:, i % 2, k, :], hot_rows(i, k),
                                     start=(k == 0), stop=False)
                pe.wait_ge(s_tablo, i + 1)
                for k in range(VK):
                    nc.tensor.matmul(pG[i % 2][:, 0, :], tab_lo[:, i % 2, k, :], hot_rows(i, k),
                                     start=False, stop=(k == VK - 1)).then_inc(s_look, 1)
                if i == 0:
                    pe.wait_ge(s_ident, 1)
                    pe.wait_ge(s_bot, 16)
                    for t in range(TILES):
                        last = nc.tensor.transpose(pT[1][:, 128 * t:128 * (t + 1)], bot[:, t, :], ident[:, :])
                    last.then_inc(s_bank, 1)
                elif i <= len(BANKS):
                    transpose_bank(0, i - 1)

            transpose_bank(1, 0)
            transpose_bank(1, 1)

            pe.wait_ge(s_lookc, LOOKED)
            gram(0, 0)
            transpose_bank(1, 2)
            transpose_bank(1, 3)
            transpose_bank(1, 4)
            gram(0, 1)
            transpose_bank(2, 0)
            transpose_bank(2, 1)

            gram(1, 0)
            layer1_bottom(0)
            gram(1, 1)
            layer1_products(0)
            transpose_bank(2, 2)
            transpose_h1(0)
            transpose_bank(2, 3)
            layer2(0)
            transpose_bank(2, 4)

            gram(2, 0)
            layer1_bottom(1)
            gram(2, 1)
            layer1_products(1)
            transpose_bank(3, 0)
            transpose_bank(3, 1)
            transpose_h1(1)
            layer2(1)
            transpose_bank(3, 2)
            layer1_bottom(2)
            layer1_products(2)
            transpose_bank(3, 3)
            transpose_bank(3, 4)
            transpose_h1(2)

            gram(3, 0)
            gram(3, 1)
            layer2(2)
            layer1_bottom(3)
            stay_busy(WAIT_MOVES)
            first, second = h1_parts(3)
            layer1_high(3, first)
            layer1_low(3, first)
            layer1_high(3, second)
            transpose_h1(3, [0])
            layer1_low(3, second)
            layer2_high(3, 0)
            transpose_h1(3, [1])
            layer2_low(3, 0)
            layer2_high(3, 1)
            layer2_low(3, 1)


def weight_rows():
    import numpy as np
    zero = FEATURES * (FEATURES - 1) // 2 + D + 1
    feature = [0] + [f + 1 for f in SLOT_TABLE[1:]]
    rows = np.full((4, 32, KTILES + 1), zero)
    place = {(f, g): ((g - FIRST) // 4, f, (g - FIRST) % 4) for g in range(FIRST, FEATURES) for f in range(g)}
    for columns, f0, f1, j, row in MOVES:
        place.update({(f, g): (j, row + f - f0, k) for k, g in enumerate(columns) for f in range(f0, min(f1, g))})
    for (f, g), at in place.items():
        a, b = sorted((feature[f], feature[g]))
        rows[at] = a * (2 * FEATURES - a - 1) // 2 + b - a - 1
    rows[BIAS_QUADRANT, BIAS_ROW, 0] = zero - 1
    rows = rows.reshape(128, KTILES + 1)
    rows[:, KTILES] = zero - 1 - D + np.arange(D)
    return rows


def kernel(**inputs):
    import numpy as np
    import concourse.bacc as bacc
    from concourse import mybir
    from concourse.bass_utils import run_bass_kernel_spmd as run

    nc = bacc.Bacc("TRN2", target_bir_lowering=False, num_devices=1)
    w1 = np.asarray(inputs["W_top1"])
    b1 = np.asarray(inputs["b_top1"])
    ids = np.asarray(inputs["ids"])
    arrays = {"bottom": inputs["r_bottom_output"], "ids": ids}
    arrays["hot_ids"] = ids.reshape(128, TILES, TABLES).transpose(2, 1, 0)[LOOKED_UP].reshape(LOOKED, B)
    arrays.update({f"tbl_{f}": inputs[f"tbl_{f}"] for f in range(TABLES)})
    arrays["w1"] = np.concatenate([w1, b1[None], np.zeros_like(b1[None])])[weight_rows()]
    arrays.update({"w2": inputs["W_top2"], "b2": inputs["b_top2"], "w3": inputs["W_top3"]})
    arrays = {name: np.ascontiguousarray(a) for name, a in arrays.items()}
    aps = {name: nc.dram_tensor(name, a.shape, mybir.dt.from_np(a.dtype), kind="ExternalInput").ap()
           for name, a in arrays.items()}
    out = nc.dram_tensor("out", (B, 1), mybir.dt.float32, kind="ExternalOutput").ap()
    tower(nc, aps["bottom"], aps["ids"], aps["hot_ids"], [aps[f"tbl_{f}"] for f in range(TABLES)],
          aps["w1"], aps["w2"], aps["b2"], aps["w3"], out)
    r = run(nc, [arrays], core_ids=[0])
    return r.results[0]["out"]
```
